# Optimizing a Trainium2 kernel written in Bass

```python
import numpy as np
import jax
import jax.numpy as jnp

def _softmax(x, axis=-1):
    return jax.nn.softmax(x, axis=axis)

def _gelu(x):
    return jax.nn.gelu(x, approximate=True)

def _silu(x):
    return jax.nn.silu(x)

def _sigmoid(x):
    return jax.nn.sigmoid(x)

def _layernorm(x, axis=-1, eps=1e-05):
    m = jnp.mean(x, axis=axis, keepdims=True)
    v = jnp.var(x, axis=axis, keepdims=True)
    return (x - m) / jnp.sqrt(v + eps)

def _scatter_add(tgt, idx, src, axis=0):
    return tgt.at[idx].add(src)

def _segment_sum(src, seg, n):
    return jax.ops.segment_sum(src, seg, n)
kernel_name = 'mk_seq_postln_d1_jaxref_r4_9c2f24'

def setup_inputs(seed: int=0):
    np.random.seed(seed)
    _w = jnp.asarray

    def _L0_attn_setup():
        import jax, jax.numpy as jnp
        import numpy as np
        D_MODEL = 256
        NUM_HEADS = 16
        BATCH = 2
        SEQ = 512

        def _trunc_normal(key, shape, std):
            return jax.random.truncated_normal(key, -3.0, 3.0, shape, dtype=jnp.float32) * std
        key = jax.random.key(seed)
        kx, kq, kk, kv, ko = jax.random.split(key, 5)
        std = (2.0 / (D_MODEL + D_MODEL)) ** 0.5
        return {'X': jax.random.normal(kx, (BATCH, SEQ, D_MODEL), dtype=jnp.float32), 'q_proj': _trunc_normal(kq, (D_MODEL, D_MODEL), std), 'k_proj': _trunc_normal(kk, (D_MODEL, D_MODEL), std), 'v_proj': _trunc_normal(kv, (D_MODEL, D_MODEL), std), 'o_proj': _trunc_normal(ko, (D_MODEL, D_MODEL), std)}
    _L0_attn_in = _L0_attn_setup()

    def _L0_ffn_setup():
        import jax, jax.numpy as jnp
        import numpy as np
        NUM_HEADS = 16
        TOP_K = 2
        key = jax.random.key(seed)
        ks = jax.random.split(key, 5)
        B, S, D, E = (4, 512, 256, 8)
        scale = 0.02
        return {'x': jax.random.normal(ks[0], (B, S, D), dtype=jnp.float32), 'W_qkv': jax.random.normal(ks[1], (D, 3 * D), dtype=jnp.float32) * scale, 'b_qkv': jnp.zeros((3 * D,), dtype=jnp.float32), 'W_gate': jax.random.normal(ks[2], (D, E), dtype=jnp.float32) * scale, 'b_gate': jnp.zeros((E,), dtype=jnp.float32), 'W_experts': jax.random.normal(ks[3], (E, D, D), dtype=jnp.float32) * scale, 'b_experts': jnp.zeros((E, D), dtype=jnp.float32)}
    _L0_ffn_in = _L0_ffn_setup()
    _d = {'L0_attn_X': _L0_attn_in['X'], 'L0_attn_q_proj': _L0_attn_in['q_proj'], 'L0_attn_k_proj': _L0_attn_in['k_proj'], 'L0_attn_v_proj': _L0_attn_in['v_proj'], 'L0_attn_o_proj': _L0_attn_in['o_proj'], 'L0_ffn_W_qkv': _L0_ffn_in['W_qkv'], 'L0_ffn_b_qkv': _L0_ffn_in['b_qkv'], 'L0_ffn_W_gate': _L0_ffn_in['W_gate'], 'L0_ffn_b_gate': _L0_ffn_in['b_gate'], 'L0_ffn_W_experts': _L0_ffn_in['W_experts'], 'L0_ffn_b_experts': _L0_ffn_in['b_experts']}
    _x0 = _d['L0_attn_X']
    _d['L0_attn_X'] = jax.random.normal(jax.random.fold_in(jax.random.key(seed), 1), (4, 2048, 256), dtype=_x0.dtype)
    del _x0
    return _d

def reference(L0_attn_X, L0_attn_q_proj, L0_attn_k_proj, L0_attn_v_proj, L0_attn_o_proj, L0_ffn_W_qkv, L0_ffn_b_qkv, L0_ffn_W_gate, L0_ffn_b_gate, L0_ffn_W_experts, L0_ffn_b_experts):

    def _L0_attn_ref(X, q_proj, k_proj, v_proj, o_proj):
        import jax, jax.numpy as jnp
        import numpy as np
        D_MODEL = 256
        NUM_HEADS = 16
        BATCH = 2
        SEQ = 512

        def _trunc_normal(key, shape, std):
            return jax.random.truncated_normal(key, -3.0, 3.0, shape, dtype=jnp.float32) * std
        B, S, D = X.shape
        H = NUM_HEADS
        d_k = D // H
        q_w = q_proj.reshape(H, d_k, D)
        k_w = k_proj.reshape(H, d_k, D)
        v_w = v_proj.reshape(H, d_k, D)
        o_w = o_proj.reshape(D, H, d_k).transpose(1, 0, 2)
        q = jnp.einsum('hkd,bsd->bhsk', q_w, X)
        k = jnp.einsum('hkd,bsd->bhsk', k_w, X)
        v = jnp.einsum('hkd,bsd->bhsk', v_w, X)
        scale = 1.0 / jnp.sqrt(jnp.asarray(d_k, dtype=X.dtype))
        scores = jnp.einsum('bhqk,bhsk->bhqs', q, k) * scale
        causal = jnp.tril(jnp.ones((S, S), dtype=bool))
        scores = jnp.where(causal, scores, jnp.asarray(-jnp.inf, dtype=scores.dtype))
        attn = jax.nn.softmax(scores, axis=-1)
        attn_out = jnp.einsum('bhqs,bhsk->bhqk', attn, v)
        return jnp.einsum('hdv,bhsv->bsd', o_w, attn_out)

    def _L0_ffn_ref(x, W_qkv, b_qkv, W_gate, b_gate, W_experts, b_experts):
        import jax, jax.numpy as jnp
        import numpy as np
        NUM_HEADS = 16
        TOP_K = 2
        B, S, D = x.shape
        H = NUM_HEADS
        hd = D // H
        E = W_gate.shape[-1]
        qkv = (x @ W_qkv + b_qkv).reshape(B, S, 3, H, hd)
        q, k, v = (qkv[:, :, 0], qkv[:, :, 1], qkv[:, :, 2])
        attn = jnp.einsum('bqhd,bkhd->bhqk', q, k) / jnp.sqrt(jnp.asarray(hd, x.dtype))
        attn = jax.nn.softmax(attn, axis=-1)
        attn_out = jnp.einsum('bhqk,bkhd->bqhd', attn, v).reshape(B, S, D)
        gate = jax.nn.softmax(x @ W_gate + b_gate, axis=-1)
        top_g, top_i = jax.lax.top_k(gate, TOP_K)
        combine = jnp.sum(jax.nn.one_hot(top_i, E, dtype=x.dtype) * top_g[..., None], axis=2)
        expert_out = jnp.einsum('bsd,edf->bsef', x, W_experts) + b_experts
        moe_out = jnp.einsum('bsef,bse->bsf', expert_out, combine)
        return attn_out + moe_out
    x = L0_attn_X
    x = _layernorm(x + _L0_attn_ref(x, L0_attn_q_proj, L0_attn_k_proj, L0_attn_v_proj, L0_attn_o_proj), axis=-1)
    x = _layernorm(x + _L0_ffn_ref(x, L0_ffn_W_qkv, L0_ffn_b_qkv, L0_ffn_W_gate, L0_ffn_b_gate, L0_ffn_W_experts, L0_ffn_b_experts), axis=-1)
    return x

_drawn_inputs = setup_inputs


def setup_inputs(seed=0):
    import zlib

    import numpy as np

    out = dict(_drawn_inputs(seed))
    spreads = {'L0_ffn_b_qkv': (0.0, 0.1), 'L0_ffn_b_gate': (0.0, 0.1), 'L0_ffn_b_experts': (0.0, 0.33)}
    factors = {'L0_ffn_W_qkv': 4.558}
    for name, (base, spread) in spreads.items():
        noise = np.random.default_rng([zlib.crc32(name.encode()), seed]).standard_normal(out[name].shape)
        drawn = base * np.exp(spread * noise) if base else spread * noise
        out[name] = jnp.asarray(drawn.astype(out[name].dtype))
    for name, factor in factors.items():
        out[name] = (out[name] * factor).astype(out[name].dtype)
    return out
```

```python
from contextlib import ExitStack

import concourse.bass as bass
import numpy as np
from concourse import mybir

F32 = mybir.dt.float32
BF16 = mybir.dt.bfloat16
I32 = mybir.dt.int32
U32 = mybir.dt.uint32
ALU = mybir.AluOpType
ACT = mybir.ActivationFunctionType
AX = mybir.AxisListType

P = 128
B, S, D = 4, 2048, 256
H, E = 16, 8
DK = D // H
G = 4
NG = H // G
QT = 512
NT = S // QT
NKB = S // P
SUB = QT // P
C = D // P
HM = P // DK
PARTS = 3
ROWS = 6 * DK
VW = DK + 1
SCALE = DK ** -0.5
EPS = 1e-5
UNDER = 16.0
SHIFT_MAX = (87.0 - 24.0 + UNDER) / 2 - UNDER
ROOT_MAX = 2.0 ** 100
MASK = -1e30
MARGIN = 1 + 1 / 64
NSC = 3
NPR = 6
N_BLOCKS = B * NT


def at(r, per, c):
    return (r + 1) * per + c


def before(u, n, ring):
    if u >= ring:
        return u - ring + 1
    last = max(v for v in range(n) if v % ring == u % ring)
    return last + 1 - n


def rounds(k, engine, n):
    return k.nc.Fori(0, n, engines=[engine], hint_back_edge=True)


def alone(engine, k):
    engine.wait_ge(k.ident_loaded, 16)


def carry(k):
    k.carried += 1
    k.nc.vector.memset(k.unused[:, k.carried:k.carried + 1], 0.0)


class Build:

    def __init__(self, nc, ctx, args, out):
        self.nc, self.ctx, self.a, self.out = nc, ctx, args, out
        self.ps = ctx.enter_context(nc.psum_tensor("ps", [P, 8, QT], F32))
        self.tok = self.sb("tok", [P, B * NKB, D], F32)
        self.ident = self.sb("ident", [P, P], F32)
        self.eps = self.sb("eps", [P, SUB], F32)
        self.mhalf = self.sb("mhalf", [P, SUB], F32)
        self.unused, self.carried = self.sb("unused", [1, 64], F32), 0
        self.flag = self.sb("flag", [1, 2], I32)
        self.qs = nc.dram_tensor("q_parts", [B, H, PARTS * DK, S], BF16).ap()
        self.ks = nc.dram_tensor("k_parts", [B, H, PARTS * DK, S], BF16).ap()
        self.ms = nc.dram_tensor("minus_shift", [B, H, S], BF16).ap()
        self.vs = nc.dram_tensor("v_ones", [B, NG, NKB, P, G * VW], F32).ap()

    def sb(self, name, shape, dt, ctx=None):
        return (ctx or self.ctx).enter_context(self.nc.sbuf_tensor(name, shape, dt))

    def sem(self, name, ctx=None):
        return self.ctx.enter_context(self.nc.semaphore(name))


def start(k):
    nc, ps = k.nc, k.ps
    loaded = k.ident_loaded = k.sem("ident_loaded")
    zeroed = k.sem("psum_zeroed")
    with nc.Block() as block:

        @block.sync
        def _(sp):
            sp.dma_start(k.ident[:, :], k.a["ident"]).then_inc(loaded, 16)
            sp.wait_ge(loaded, 16)

        @block.vector
        def _(dve):
            for n in range(8):
                nc.vector.memset(ps[:, n, :], 0.0).then_inc(zeroed, 1)
            nc.vector.memset(k.eps[:, :], EPS).then_inc(zeroed, 1)
            nc.vector.memset(k.mhalf[:, :], -0.5).then_inc(zeroed, 1)
            nc.vector.memset(k.flag[:, :], 0).then_inc(zeroed, 1)
            dve.wait_ge(zeroed, 11)


class Projection:

    def __init__(self, k, ctx, layer):
        self.k, self.layer = k, layer
        sb = lambda name, shape, dt: k.sb(f"{name}{layer}", shape, dt, ctx)
        sem = lambda name: k.sem(f"{name}_{layer}")
        self.wqk = sb("wqk", [P, C, 2 * D], F32)
        self.wv = sb("wv", [P, C, D], F32)
        self.sums = sb("sums", [P, 32], BF16)
        self.bias = sb("bias", [P, 4], F32)
        self.qf = sb("qf", [P, 4, QT], F32)
        self.part = sb("part", [P, 4, PARTS, QT], BF16)
        self.rest = sb("rest", [P, 2, QT], F32)
        self.sq = sb("sq", [P, 4, QT], BF16)
        self.v = sb("v", [P, SUB, H, VW], F32)
        self.qn = sb("qn", [40, S], F32)
        self.kn = sb("kn", [40, NT], F32)
        self.kmax = sb("kmax", [40, 1], F32)
        self.mshift = sb("mshift", [40, S], BF16)
        self.least = sb("least", [40, B], F32)
        self.least_row = sb("least_row", [1, B * H], F32)
        self.least1 = sb("least1", [1, 1], F32)
        self.consts = sem("weights_loaded")
        self.set = sem("ones_set")
        self.qk_ready = sem("qk_ready")
        self.qk_copied = sem("qk_copied")
        self.part_ready = sem("part_ready")
        self.sq_ready = sem("sq_ready")
        self.split = sem("split")
        self.stored_part = [sem(f"stored_part{n}") for n in range(4)]
        self.v_ready = sem("v_ready")
        self.v_copied = sem("v_copied")
        self.stored_v = sem("stored_v")
        self.norm_ready = sem("norm_ready")
        self.norm_read = sem("norm_read")
        self.shift_step = sem("shift_step")
        self.root_ready = sem("root_ready")
        self.stored_shift = sem("stored_shift")

    def sp_consts(self, sp):
        k, l = self.k, self.layer
        a = k.a
        sp.dma_start(self.wqk[:, :, :], a[f"wqk{l}"].rearrange("(c p) n -> p c n", p=P)).then_inc(self.consts, 16)
        sp.dma_start(self.wv[:, :, :], a[f"wv{l}"].rearrange("(c p) n -> p c n", p=P)).then_inc(self.consts, 16)
        sp.dma_start(self.sums[:, :], a["sums"]).then_inc(self.consts, 16)
        if l == 2:
            with self.k.nc.allow_non_contiguous_dma(reason="a bias per partition"):
                sp.dma_start(self.bias[:, :], a["b_qkv"][0:2 * D].rearrange("(n p) -> p n", p=P)).then_inc(self.consts, 16)
        self.n_consts = 64 if l == 2 else 48

    def pe_tiles(self, pe, r, t, xt):
        nc, ps = self.k.nc, self.k.ps
        for n in range(4):
            pe.wait_ge(self.qk_copied, at(r, 4 * NT, 4 * (t - 1) + n + 1))
            for c in range(C):
                last = nc.tensor.matmul(ps[:, n, :], self.wqk[:, c, n * P:(n + 1) * P], xt[:, c, :],
                                        start=c == 0, stop=c == C - 1)
            last.then_inc(self.qk_ready, 1)

    def pe_v(self, pe, r, t, xt):
        nc, ps = self.k.nc, self.k.ps
        for b in range(2):
            pe.wait_ge(self.v_copied, at(r, 2 * NT, 2 * (t - 1) + b + 1))
            for s in range(2):
                for c in range(C):
                    last = nc.tensor.matmul(ps[:, 4 + b, s * D:(s + 1) * D],
                                            xt[:, c, (2 * b + s) * P:(2 * b + s + 1) * P], self.wv[:, c, :],
                                            start=c == 0, stop=c == C - 1)
            last.then_inc(self.v_ready, 1)

    def pe_norms(self, pe, r, t):
        nc, ps = self.k.nc, self.k.ps
        pe.wait_ge(self.norm_read, at(r, 2 * NT, 2 * t))
        for n in range(4):
            pe.wait_ge(self.sq_ready, at(r, 4 * NT, 4 * t + n + 1))
            row = 32 * (n % 2)
            last = nc.tensor.matmul(ps[row:row + 32, 7 - n // 2, :], self.sums[:, :],
                                    self.sq[:, n, :], start=True, stop=True)
        last.then_inc(self.norm_ready, 1)

    def act_tiles(self, act, r, t):
        nc, ps = self.k.nc, self.k.ps
        for n in range(4):
            act.wait_ge(self.qk_ready, at(r, 4 * NT, 4 * t + n + 1))
            act.wait_ge(self.split, at(r, 12 * NT, 12 * (t - 1) + 3 * n + 1))
            bias = self.bias[:, n:n + 1] if self.layer == 2 else 0.0
            nc.scalar.activation(self.qf[:, n, :], ps[:, n, :], ACT.Identity, bias=bias).then_inc(self.qk_copied, 1)
            act.wait_ge(self.qk_copied, at(r, 4 * NT, 4 * t + n + 1))
            act.wait_ge(self.stored_part[n], at(r, 48 * NT, 48 * t))
            nc.scalar.activation(self.part[:, n, 0, :], self.qf[:, n, :], ACT.Copy).then_inc(self.part_ready, 1)
            if n == 0:
                act.wait_ge(self.norm_ready, at(r, NT, t))
            nc.scalar.activation(self.sq[:, n, :], self.qf[:, n, :], ACT.Square).then_inc(self.sq_ready, 1)

    def act_v(self, act, r, t):
        nc, ps = self.k.nc, self.k.ps
        for b in range(2):
            act.wait_ge(self.v_ready, at(r, 2 * NT, 2 * t + b + 1))
            if b == 0:
                act.wait_ge(self.stored_v, at(r, 64 * NT, 64 * t))
            for s in range(2):
                last = nc.scalar.activation(self.v[:, 2 * b + s, :, 0:DK],
                                            ps[:, 4 + b, s * D:(s + 1) * D].rearrange("p (h e) -> p h e", e=DK), ACT.Copy)
            last.then_inc(self.v_copied, 1)

    def dve_v(self, dve, r, t, bias):
        nc, ps = self.k.nc, self.k.ps
        for b in range(2):
            dve.wait_ge(self.v_ready, at(r, 2 * NT, 2 * t + b + 1))
            if b == 0:
                dve.wait_ge(self.stored_v, at(r, 64 * NT, 64 * t))
            for s in range(2):
                last = nc.vector.tensor_tensor(self.v[:, 2 * b + s, :, 0:DK],
                                               ps[:, 4 + b, s * D:(s + 1) * D].rearrange("p (h e) -> p h e", e=DK),
                                               bias[:, :].rearrange("p (h e) -> p h e", e=DK), ALU.add)
            last.then_inc(self.v_copied, 1)

    def dve_split(self, dve, r, t):
        nc = self.k.nc
        for n in range(4):
            rest = self.rest[:, n % 2, :]
            step = lambda c: at(r, 12 * NT, 12 * t + 3 * n + c)
            dve.wait_ge(self.part_ready, at(r, 4 * NT, 4 * t + n + 1))
            dve.wait_ge(self.split, step(-3))
            nc.vector.tensor_tensor(rest, self.qf[:, n, :], self.part[:, n, 0, :], ALU.subtract).then_inc(self.split, 1)
            dve.wait_ge(self.split, step(1))
            nc.vector.tensor_copy(self.part[:, n, 1, :], rest).then_inc(self.split, 1)
            dve.wait_ge(self.split, step(2))
            nc.vector.tensor_tensor(self.part[:, n, 2, :], rest, self.part[:, n, 1, :], ALU.subtract).then_inc(self.split, 1)

    def dve_norms(self, dve, r, t):
        nc, ps = self.k.nc, self.k.ps
        dve.wait_ge(self.norm_ready, at(r, NT, t + 1))
        if t == 0:
            dve.wait_ge(self.shift_step, at(r, 4, 0))
        nc.vector.tensor_copy(self.qn[:, t * QT:(t + 1) * QT], ps[0:40, 7, :]).then_inc(self.norm_read, 1)
        nc.vector.tensor_reduce(self.kn[:, t:t + 1], ps[0:40, 6, :], AX.X, ALU.max).then_inc(self.norm_read, 1)
        if t == NT - 1:
            dve.wait_ge(self.norm_read, at(r, 2 * NT, 2 * NT))
            nc.vector.tensor_reduce(self.kmax[:, :], self.kn[:, :], AX.X, ALU.max).then_inc(self.shift_step, 1)
            dve.wait_ge(self.shift_step, at(r, 4, 1))
            nc.vector.tensor_scalar(self.qn[:, :], self.qn[:, :], self.kmax[:, 0:1], ROOT_MAX, ALU.mult,
                                    ALU.min).then_inc(self.shift_step, 1)

    def act_root(self, act, r):
        act.wait_ge(self.shift_step, at(r, 4, 2))
        self.k.nc.scalar.activation(self.qn[:, :], self.qn[:, :], ACT.Sqrt).then_inc(self.root_ready, 1)

    def dve_shift(self, dve, r):
        nc = self.k.nc
        dve.wait_ge(self.root_ready, at(r, 1, 1))
        dve.wait_ge(self.stored_shift, at(r, 32, 0))
        nc.vector.tensor_scalar(self.mshift[:, :], self.qn[:, :], -1.0, UNDER / SCALE, ALU.mult,
                                ALU.add).then_inc(self.shift_step, 1)
        dve.wait_ge(self.shift_step, at(r, 4, 3))
        nc.vector.tensor_reduce(self.least[:, bass.ds(r, 1)], self.mshift[:, :], AX.X, ALU.min).then_inc(self.shift_step, 1)

    def sp_store(self, sp, r, t):
        k = self.k
        for n in range(4):
            dst = (k.qs, k.ks)[n // 2]
            alone(sp, k)
            sp.wait_ge(self.split, at(r, 12 * NT, 12 * t + 3 * n + 3))
            for part in range(PARTS):
                to = dst[bass.ds(r, 1), HM * (n % 2):HM * (n % 2) + HM, part * DK:(part + 1) * DK, t * QT:(t + 1) * QT]
                sp.dma_start(to.rearrange("b h i s -> (b h) i s"), self.part[:, n, part, :]).then_inc(self.stored_part[n], 16)
        for s in range(SUB):
            alone(sp, k)
            sp.wait_ge(self.v_copied, at(r, 2 * NT, 2 * t + s // 2 + 1))
            to = k.vs[bass.ds(r, 1), :, t * SUB + s, :, :].rearrange("b g p e -> p (b g) e")
            sp.dma_start(to, self.v[:, s, :, :].rearrange("p (g j) e -> p g (j e)", g=NG)).then_inc(self.stored_v, 16)
        if t == NT - 1:
            alone(sp, k)
            sp.wait_ge(self.shift_step, at(r, 4, 3))
            for m in range(2):
                to = k.ms[bass.ds(r, 1), m * HM:(m + 1) * HM, :].rearrange("b h s -> (b h) s")
                sp.dma_start(to, self.mshift[32 * m:32 * m + HM, :]).then_inc(self.stored_shift, 16)

    def lead(self, engine, which):
        per = {"pe": ((self.qk_ready, 4 * NT), (self.v_ready, 2 * NT), (self.norm_ready, NT)),
               "act": ((self.root_ready, 1), (self.qk_copied, 4 * NT), (self.part_ready, 4 * NT), (self.sq_ready, 4 * NT)),
               "dve": ((self.split, 12 * NT), (self.norm_read, 2 * NT), (self.shift_step, 4)),
               "sp": tuple((x, 48 * NT) for x in self.stored_part) + ((self.stored_v, 64 * NT), (self.stored_shift, 32))}
        for s, n in per[which]:
            engine.sem_inc(s, n)

    def sp_end(self, sp):
        for x in self.stored_part:
            sp.wait_ge(x, at(B - 1, 48 * NT, 48 * NT))
        sp.wait_ge(self.stored_v, at(B - 1, 64 * NT, 64 * NT))
        sp.wait_ge(self.stored_shift, at(B - 1, 32, 32))
        sp.wait_ge(self.shift_step, at(B - 1, 4, 4))
        gathered = self.gathered = self.k.sem(f"least_gathered_{self.layer}")
        with self.k.nc.allow_non_contiguous_dma(reason="one number per head and batch"):
            for m in range(2):
                sp.dma_start(self.least_row[0:1, m * B * HM:(m + 1) * B * HM],
                             self.least[32 * m:32 * m + HM, :]).then_inc(gathered, 16)

    def dve_flag(self, dve):
        nc = self.k.nc
        step = self.k.sem(f"flag_step_{self.layer}")
        dve.wait_ge(self.gathered, 32)
        nc.vector.tensor_reduce(self.least1[:, :], self.least_row[:, :], AX.X, ALU.min).then_inc(step, 1)
        dve.wait_ge(step, 1)
        nc.vector.tensor_scalar(self.k.flag[:, self.layer - 1:self.layer], self.least1[:, :], -SHIFT_MAX / SCALE, None,
                                ALU.is_lt).then_inc(step, 1)
        dve.wait_ge(step, 2)


def project(k):
    nc = k.nc
    with ExitStack() as ctx:
        pr = Projection(k, ctx, 1)
        xt = k.sb("xt", [P, 2, C, QT], F32, ctx)
        x_loaded = [k.sem(f"x_loaded{p}") for p in range(2)]
        half = NT // 2
        with nc.Block() as block:

            @block.sync
            def _(sp):
                pr.sp_consts(sp)
                pr.lead(sp, "sp")
                for s in x_loaded:
                    sp.sem_inc(s, 16 * half)
                with rounds(k, mybir.EngineType.SP, B) as r:
                    for t in range(NT):
                        alone(sp, k)
                        sp.wait_ge(pr.v_ready, at(r, 2 * NT, 2 * (t - 1)))
                        src = k.a["xt"][bass.ds(r, 1), :, t * QT:(t + 1) * QT].rearrange("b (c p) s -> p (b c) s", p=P)
                        sp.dma_start(xt[:, t % 2, :, :], src).then_inc(x_loaded[t % 2], 16)
                        if t > 0:
                            pr.sp_store(sp, r, t - 1)
                    pr.sp_store(sp, r, NT - 1)
                pr.sp_end(sp)

            @block.tensor
            def _(pe):
                pr.lead(pe, "pe")
                pe.wait_ge(pr.consts, pr.n_consts)
                with rounds(k, mybir.EngineType.PE, B) as r:
                    for t in range(NT):
                        pe.wait_ge(x_loaded[t % 2], at(r, 16 * half, 16 * (t // 2 + 1)))
                        pr.pe_tiles(pe, r, t, xt[:, t % 2, :, :])
                        pr.pe_v(pe, r, t, xt[:, t % 2, :, :])
                        pr.pe_norms(pe, r, t)

            @block.scalar
            def _(act):
                pr.lead(act, "act")
                act.sem_inc(pr.v_copied, 2 * NT)
                act.wait_ge(pr.set, 1)
                with rounds(k, mybir.EngineType.Activation, B) as r:
                    for t in range(NT):
                        pr.act_tiles(act, r, t)
                        pr.act_v(act, r, t)
                    pr.act_root(act, r)

            @block.vector
            def _(dve):
                pr.lead(dve, "dve")
                nc.vector.memset(pr.v[:, :, :, DK:VW], 1.0).then_inc(pr.set, 1)
                with rounds(k, mybir.EngineType.DVE, B) as r:
                    for t in range(NT):
                        pr.dve_split(dve, r, t)
                        pr.dve_norms(dve, r, t)
                    pr.dve_shift(dve, r)
                pr.dve_flag(dve)


def row_max(k, layer):
    nc, ps = k.nc, k.ps
    causal = layer == 1
    R = B * H
    NQ = S // P
    chunks = lambda n: n // SUB + 1 if causal else NT
    with ExitStack() as ctx:
        sb = lambda name, shape, dt: k.sb(f"max_{name}{layer}", shape, dt, ctx)
        sem = lambda name: k.sem(f"max_{name}_{layer}")
        qst = sb("q", [ROWS, S], BF16)
        kst = sb("k", [ROWS, S], BF16)
        mask = sb("mask", [P, SUB, QT], F32)
        masked = sb("masked", [P, 2, QT], F32)
        part = sb("part", [P, NQ, NT], F32)
        biggest = sb("biggest", [P, NQ], F32)
        row = sb("row", [NQ, P], BF16)
        loaded, masks = sem("loaded"), sem("mask_loaded")
        cleared = sem("cleared")
        ready = sem("ready")
        read = sem("read")
        step = sem("step")
        turned = sem("turned")
        stored = sem("stored")
        on_mask = sem("on_mask")
        ND = 9
        qs_f = k.qs.rearrange("b h i s -> (b h) i s")
        ks_f = k.ks.rearrange("b h i s -> (b h) i s")
        ms_f = k.ms.rearrange("b h (n p) -> (b h) n p", p=P)

        def taken(engine):
            return engine.value_load(k.flag[0:1, layer - 1:layer], min_val=0, max_val=1)

        with nc.Block() as block:

            @block.sync
            def _(sp):
                with sp.If(taken(sp) > 0):
                    sp.dma_start(mask[:, :, :], k.a["mask_wide"]).then_inc(masks, 16)
                    sp.sem_inc(loaded, 16 * ND)
                    sp.sem_inc(stored, 16)
                    with rounds(k, mybir.EngineType.SP, R) as r:
                        alone(sp, k)
                        sp.wait_ge(read, at(r, NQ, 0))
                        at_row = 0
                        for n in (3, 2, 1):
                            src = qs_f[bass.ds(r, 1), 0:n * DK, :].rearrange("h i s -> (h i) s")
                            sp.dma_start(qst[at_row:at_row + n * DK, :], src).then_inc(loaded, 16)
                            part_k = 3 - n
                            for _ in range(n):
                                src = ks_f[bass.ds(r, 1), part_k * DK:(part_k + 1) * DK, :].rearrange("h i s -> (h i) s")
                                sp.dma_start(kst[at_row:at_row + DK, :], src).then_inc(loaded, 16)
                                at_row += DK
                        alone(sp, k)
                        sp.wait_ge(step, at(r, 2, 2))
                        sp.dma_start(ms_f[bass.ds(r, 1), :, :].rearrange("h n p -> (h n) p"), row[:, :]).then_inc(stored, 16)
                    sp.wait_ge(stored, 16 * (R + 1))

            @block.tensor
            def _(pe):
                with pe.If(taken(pe) > 0):
                    pe.sem_inc(ready, NQ)
                    pe.sem_inc(turned, 1)
                    with rounds(k, mybir.EngineType.PE, R) as r:
                        pe.wait_ge(loaded, at(r, 16 * ND, 16 * ND))
                        for n in range(NQ):
                            pe.wait_ge(read, at(r, NQ, n - 1))
                            if n == 0:
                                pe.wait_ge(step, at(r, 2, 0))
                            for c in range(chunks(n)):
                                last = nc.tensor.matmul(ps[:, 4 * (n % 2) + c, :], qst[:, n * P:(n + 1) * P],
                                                        kst[:, c * QT:(c + 1) * QT], start=True, stop=True)
                            last.then_inc(ready, 1)
                        pe.wait_ge(step, at(r, 2, 1))
                        nc.tensor.transpose(ps[0:NQ, 0, 0:P], biggest[:, :], k.ident[:, :]).then_inc(turned, 1)

            @block.vector
            def _(dve):
                with dve.If(taken(dve) > 0):
                    nc.vector.memset(part[:, :, :], -3e38).then_inc(cleared, 1)
                    dve.sem_inc(read, NQ)
                    dve.sem_inc(step, 2)
                    dve.sem_inc(on_mask, NQ)
                    dve.wait_ge(cleared, 1)
                    dve.wait_ge(masks, 16)
                    with rounds(k, mybir.EngineType.DVE, R) as r:
                        for n in range(NQ):
                            full = chunks(n) - (1 if causal else 0)
                            dve.wait_ge(ready, at(r, NQ, n + 1))
                            if n == 0:
                                dve.wait_ge(step, at(r, 2, 0))
                            bank = 4 * (n % 2)
                            if causal:
                                dve.wait_ge(read, at(r, NQ, n - 1))
                                nc.vector.tensor_tensor(masked[:, n % 2, :], ps[:, bank + full, :], mask[:, n % SUB, :],
                                                        ALU.add).then_inc(on_mask, 1)
                            if full:
                                last = nc.vector.tensor_reduce(part[:, n, 0:full], ps[:, bank:bank + full, :], AX.X, ALU.max)
                            if causal:
                                dve.wait_ge(on_mask, at(r, NQ, n + 1))
                                last = nc.vector.tensor_reduce(part[:, n, full:full + 1], masked[:, n % 2, :], AX.X, ALU.max)
                            last.then_inc(read, 1)
                        dve.wait_ge(read, at(r, NQ, NQ))
                        dve.wait_ge(turned, at(r, 1, 0))
                        nc.vector.tensor_reduce(biggest[:, :], part[:, :, :], AX.X, ALU.max).then_inc(step, 1)
                        dve.wait_ge(turned, at(r, 1, 1))
                        dve.wait_ge(stored, at(r, 16, 0))
                        nc.vector.tensor_scalar(row[:, :], ps[0:NQ, 0, 0:P], -1.0, None, ALU.mult).then_inc(step, 1)
                    dve.wait_ge(step, at(R - 1, 2, 2))


def attend(k, layer):
    nc, ps = k.nc, k.ps
    causal = layer == 1
    quads = [(t, kb) for t in range(NT) for kb in range((t + 1) * SUB if causal else NKB)]
    NQ = len(quads)
    NH = 2 * NQ
    last_quad = [max(n for n, (t, _) in enumerate(quads) if t == u) for u in range(NT)]
    last_of_chunk = [max(n for n, (_, kb) in enumerate(quads) if kb // SUB == c) for c in range(NT)]
    R = B * NG
    off = lambda t, kb: max(0, kb - SUB * t) * P if causal else 0
    with ExitStack() as ctx:
        sb = lambda name, shape, dt: k.sb(f"{name}{layer}", shape, dt, ctx)
        sem = lambda name: k.sem(f"{name}_{layer}")
        qst = sb("q_stack", [ROWS + 1, G, S], BF16)
        kst = sb("k_stack", [ROWS + 1, G, S], BF16)
        vt = sb("v_keys", [P, NKB, G, VW], F32)
        prob = sb("prob", [P, NPR, 2, QT], F32)
        o_sb = sb("o_sb", [P, 2, QT], F32)
        rs = sb("rs", [P, 2, SUB, G], F32)
        o_n = sb("o_n", [P, 2, SUB, G, DK], F32)
        mask = sb("mask", [P, P], BF16)
        identb = sb("identb", [P, P], BF16)
        warm = sb("warm", [P, 1], F32)
        warmed = sem("warmed")
        consts = sem("mask_loaded")
        ones_set = sem("k_ones_set")
        q_loaded = [sem(f"q_loaded{t}") for t in range(NT)]
        kv_loaded = [sem(f"kv_loaded{c}") for c in range(NT)]
        scores_ready = sem("scores_ready")
        probs_ready = sem("probs_ready")
        pv_done = sem("pv_done")
        o_copied = sem("o_copied")
        o_turned = sem("o_turned")
        o_read = sem("o_read")

        def load_q(sp, r, t):
            for row, n in ((0, 3), (3 * DK, 2), (5 * DK, 1)):
                src = qs_f[bass.ds(r * G, G), 0:n * DK, t * QT:(t + 1) * QT].rearrange("h i s -> i h s")
                sp.dma_start(qst[row:row + n * DK, :, t * QT:(t + 1) * QT], src).then_inc(q_loaded[t], 16)
            src = ms_f[bass.ds(r * G, G), t * QT:(t + 1) * QT].rearrange("(o h) s -> o h s", o=1)
            sp.dma_start(qst[ROWS:ROWS + 1, :, t * QT:(t + 1) * QT], src).then_inc(q_loaded[t], 16)

        def load_kv(sp, r, c):
            row = 0
            for part, n in ((0, 3), (1, 2), (2, 1)):
                for _ in range(n):
                    src = ks_f[bass.ds(r * G, G), part * DK:(part + 1) * DK, c * QT:(c + 1) * QT].rearrange("h i s -> i h s")
                    sp.dma_start(kst[row:row + DK, :, c * QT:(c + 1) * QT], src).then_inc(kv_loaded[c], 16)
                    row += DK
            src = vs_f[bass.ds(r, 1), c * SUB:(c + 1) * SUB, :, :].rearrange("b n p e -> p (b n) e")
            sp.dma_start(vt[:, c * SUB:(c + 1) * SUB, :, :].rearrange("p n j e -> p n (j e)"), src).then_inc(kv_loaded[c], 16)

        qs_f = k.qs.rearrange("b h i s -> (b h) i s")
        ks_f = k.ks.rearrange("b h i s -> (b h) i s")
        ms_f = k.ms.rearrange("b h s -> (b h) s")
        vs_f = k.vs.rearrange("b g n p e -> (b g) n p e")
        NQD, NKD = 4, 7
        OSTEPS = 3 if layer == 2 else 2

        with nc.Block() as block:

            @block.sync
            def _(sp):
                sp.dma_start(identb[:, :], k.a["identb"]).then_inc(consts, 16)
                sp.dma_start(mask[:, :], k.a["mask"]).then_inc(consts, 16)
                for s in q_loaded:
                    sp.sem_inc(s, 16 * NQD)
                for s in kv_loaded:
                    sp.sem_inc(s, 16 * NKD)
                with rounds(k, mybir.EngineType.SP, R) as r:
                    for t in range(NT):
                        if t == NT - 1:
                            for c in range(NT):
                                alone(sp, k)
                                sp.wait_ge(pv_done, at(r, NQ, last_of_chunk[c] + 1 - NQ))
                                load_kv(sp, r, c)
                        alone(sp, k)
                        sp.wait_ge(pv_done, at(r, NQ, last_quad[t] + 1 - NQ))
                        load_q(sp, r, t)

            @block.tensor
            def _(pe):
                pe.sem_inc(scores_ready, NH)
                pe.sem_inc(pv_done, NQ)
                pe.sem_inc(o_turned, NT)
                pe.wait_ge(consts, 32)
                pe.wait_ge(ones_set, 1)

                def scores(r, u):
                    n, half = u // 2, u % 2
                    t, kb = quads[n]
                    w0 = off(t, kb)
                    if kb == 0 and half == 0:
                        pe.wait_ge(q_loaded[t], at(r, 16 * NQD, 16 * NQD))
                    if t == (kb // SUB if causal else 0) and kb % SUB == 0 and half == 0:
                        pe.wait_ge(kv_loaded[kb // SUB], at(r, 16 * NKD, 16 * NKD))
                    pe.wait_ge(probs_ready, at(r, NH, before(u, NH, NSC)))
                    for j in (2 * half, 2 * half + 1):
                        bank = 2 * (u % NSC) + j % 2
                        diagonal = causal and kb >= SUB * t
                        last = nc.tensor.matmul(ps[:, bank, w0:QT], kst[:, j, kb * P:(kb + 1) * P],
                                                qst[:, j, t * QT + w0:(t + 1) * QT], start=True, stop=not diagonal)
                        if diagonal:
                            last = nc.tensor.matmul(ps[:, bank, w0:w0 + P], identb[:, :], mask[:, :],
                                                    start=False, stop=True)
                    last.then_inc(scores_ready, 1)

                def values(r, n):
                    t, kb = quads[n]
                    w0 = off(t, kb)
                    if kb == 0:
                        pe.wait_ge(o_read, at(r, OSTEPS * NT, OSTEPS * (t - 1)))
                    pe.wait_ge(probs_ready, at(r, NH, 2 * n + 2))
                    for j in range(G):
                        last = nc.tensor.matmul(ps[32 * j:32 * j + VW, 6 + t % 2, w0:QT], vt[:, kb, j, :],
                                                prob[:, (2 * n + j // 2) % NPR, j % 2, w0:QT],
                                                start=kb == 0, stop=n == last_quad[t])
                    last.then_inc(pv_done, 1)

                def turn(r, t):
                    pe.wait_ge(o_copied, at(r, NT, t + 1))
                    for s in range(SUB):
                        last = nc.tensor.transpose(ps[:, 6 + t % 2, s * P:(s + 1) * P], o_sb[:, t % 2, s * P:(s + 1) * P],
                                                   k.ident[:, :])
                    last.then_inc(o_turned, 1)

                with rounds(k, mybir.EngineType.PE, R) as r:
                    for u in range(NSC):
                        scores(r, u)
                    for n in range(NQ):
                        for u in range(2 * n + NSC, min(2 * n + NSC + 2, NH)):
                            scores(r, u)
                        values(r, n)
                        t, kb = quads[n]
                        if t and kb == 1:
                            turn(r, t - 1)
                    turn(r, NT - 1)

            @block.scalar
            def _(act):
                act.sem_inc(probs_ready, NH)
                nc.scalar.activation(warm[:, :], k.eps[:, 0:1], ACT.Exp).then_inc(warmed, 1)
                act.wait_ge(warmed, 1)
                with rounds(k, mybir.EngineType.Activation, R) as r:
                    for n, (t, kb) in enumerate(quads):
                        w0 = off(t, kb)
                        for half in range(2):
                            u = 2 * n + half
                            act.wait_ge(pv_done, at(r, NQ, (before(u, NH, NPR) + 1) // 2))
                            act.wait_ge(scores_ready, at(r, NH, u + 1))
                            sc = 2 * (u % NSC)
                            nc.scalar.activation(prob[:, u % NPR, :, w0:QT], ps[:, sc:sc + 2, w0:QT],
                                                 ACT.Exp, scale=SCALE).then_inc(probs_ready, 1)

            @block.vector
            def _(dve):
                nc.vector.memset(kst[ROWS:ROWS + 1, :, :], 1.0).then_inc(ones_set, 1)
                dve.sem_inc(o_copied, NT)
                dve.sem_inc(o_read, OSTEPS * NT)

                def normalise(r, b, g, t):
                    dve.wait_ge(o_turned, at(r, NT, t + 1))
                    o = ps[:, 6 + t % 2, :].rearrange("p (s j e) -> p s j e", s=SUB, j=G)
                    step = lambda c: at(r, OSTEPS * NT, OSTEPS * t + c)
                    nc.vector.reciprocal(rs[:, t % 2, :, :], o[:, :, :, DK]).then_inc(o_read, 1)
                    dve.wait_ge(o_read, step(1))
                    to = k.tok[:, bass.ds(b * NKB + t * SUB, SUB), bass.ds(g * G * DK, G * DK)]
                    dst = to.rearrange("p s (j e) -> p s j e", j=G) if layer == 1 else o_n[:, t % 2, :, :, :]
                    nc.vector.tensor_tensor(dst, o[:, :, :, 0:DK],
                                            rs[:, t % 2, :, :].unsqueeze(3).to_broadcast([P, SUB, G, DK]),
                                            ALU.mult).then_inc(o_read, 1)
                    if layer == 2:
                        dve.wait_ge(o_read, step(2))
                        nc.vector.tensor_tensor(to, o_n[:, t % 2, :, :, :].rearrange("p s j e -> p s (j e)"), to,
                                                ALU.add).then_inc(o_read, 1)

                with rounds(k, mybir.EngineType.DVE, B) as b:
                    with rounds(k, mybir.EngineType.DVE, NG) as g:
                        r = b * NG + g
                        for t in range(NT):
                            dve.wait_ge(pv_done, at(r, NQ, last_quad[t] + 1))
                            dve.wait_ge(o_turned, at(r, NT, t - 1))
                            nc.vector.tensor_copy(o_sb[:, t % 2, :], ps[:, 6 + t % 2, :]).then_inc(o_copied, 1)
                            normalise(r, b, g, t)


def middle(k):
    nc, ps = k.nc, k.ps
    a = k.a
    with ExitStack() as ctx:
        pr = Projection(k, ctx, 2)
        sb = lambda name, shape, dt: k.sb(name, shape, dt, ctx)
        wo = sb("wo", [P, C, D], F32)
        wg = sb("wg", [P, C, E], F32)
        we = sb("we", [P, C, E * D], F32)
        be = sb("be", [E, D], F32)
        bv = sb("bv", [P, D], F32)
        bg = sb("bg", [P, SUB, E], F32)
        iota = sb("iota", [P, E], F32)
        xr = sb("xr", [P, 2, SUB, D], F32)
        att = sb("att", [P, SUB, D], F32)
        att_t = sb("att_t", [P, C, QT], F32)
        x1 = sb("x1", [P, 2, SUB, D], F32)
        x1t = sb("x1t", [P, C, QT], F32)
        stats = sb("stats", [P, SUB, 6], F32)
        mv = sb("mv", [P, SUB, 2], F32)
        rstd = sb("rstd", [P, 2, SUB], F32)
        logit = sb("logit", [P, SUB, E], F32)
        small = sb("small", [P, SUB, 4], F32)
        expd = sb("expd", [P, SUB, E], F32)
        gate = sb("gate", [P, SUB, E], F32)
        top = sb("top", [P, SUB, E], F32)
        topi = sb("topi", [P, SUB, E], U32)
        topf = sb("topf", [P, SUB, E], F32)
        hot = sb("hot", [P, SUB, E], F32)
        comb = sb("comb", [P, 2, SUB, E], F32)
        comb_t = sb("comb_t", [E, QT], F32)
        consts = k.sem("middle_consts")
        x_loaded = [k.sem(f"residual_loaded{p}") for p in range(2)]
        att_copied = k.sem("att_copied")
        att_turned = k.sem("att_turned")
        att_t_copied = k.sem("att_t_copied")
        o_ready = k.sem("o_ready")
        o_added = k.sem("o_added")
        ln_step = k.sem("ln_step")
        rstd_ready = k.sem("rstd_ready")
        x1_ready = k.sem("x1_ready")
        x1_turned = k.sem("x1_turned")
        x1t_copied = k.sem("x1t_copied")
        gate_ready = k.sem("gate_ready")
        gate_step = k.sem("gate_step")
        exp_ready = k.sem("exp_ready")
        comb_turned = k.sem("comb_turned")
        comb_copied = k.sem("comb_copied")
        be_ready = k.sem("be_ready")
        be_added = k.sem("be_added")
        exp_tile = k.sem("expert_tile")
        exp_added = k.sem("expert_added")
        half = NT // 2
        GS = 12 + 2 * SUB
        NE = E // 2
        with nc.Block() as block:

            @block.sync
            def _(sp):
                pr.sp_consts(sp)
                for dst, src in ((wo[:, :, :], a["wo"].rearrange("(c p) n -> p c n", p=P)),
                                 (wg[:, :, :], a["wg"].rearrange("(c p) n -> p c n", p=P)),
                                 (be[:, :], a["b_exp"]),
                                 (bv[:, :], a["b_qkv"][2 * D:3 * D].rearrange("(o n) -> o n", o=1).to_broadcast([P, D])),
                                 (iota[:, :], a["iota"])):
                    sp.dma_start(dst, src).then_inc(consts, 16)
                for c in range(C):
                    sp.dma_start(we[:, c, :].rearrange("p (e n) -> p e n", e=E),
                                 a["w_exp"][:, c * P:(c + 1) * P, :].rearrange("e p n -> p e n")).then_inc(consts, 16)
                for s in range(SUB):
                    sp.dma_start(bg[:, s, :], a["b_gate"].rearrange("(o n) -> o n", o=1).to_broadcast([P, E])).then_inc(consts, 16)
                pr.lead(sp, "sp")
                for s in x_loaded:
                    sp.sem_inc(s, 16 * half)
                with rounds(k, mybir.EngineType.SP, B) as r:
                    for t in range(NT):
                        alone(sp, k)
                        sp.wait_ge(x1_ready, at(r, SUB * NT, SUB * (t - 1)))
                        src = a["x"][bass.ds(r, 1), t * QT:(t + 1) * QT, :].rearrange("b (s p) d -> p (b s) d", p=P)
                        sp.dma_start(xr[:, t % 2, :, :], src).then_inc(x_loaded[t % 2], 16)
                        if t > 0:
                            pr.sp_store(sp, r, t - 1)
                    pr.sp_store(sp, r, NT - 1)
                pr.sp_end(sp)

            @block.gpsimd
            def _(pool):
                pool.sem_inc(att_copied, NT)
                pool.sem_inc(rstd_ready, 2 * NT)

                def copy_att(r, t):
                    pool.wait_ge(att_turned, at(r, NT, t))
                    nc.gpsimd.tensor_copy(att[:, :, :], k.tok[:, bass.ds(r * NKB + t * SUB, SUB), :]).then_inc(att_copied, 1)

                with rounds(k, mybir.EngineType.Pool, B) as r:
                    copy_att(r, 0)
                    for t in range(NT):
                        if t + 1 < NT:
                            copy_att(r, t + 1)
                        pool.wait_ge(ln_step, at(r, 8 * NT, 8 * t + 8))
                        nc.gpsimd.tensor_tensor(rstd[:, 1, :], mv[:, :, 1], k.eps[:, :], ALU.add).then_inc(rstd_ready, 1)
                        pool.wait_ge(rstd_ready, at(r, 2 * NT, 2 * t + 1))
                        pool.wait_ge(x1_ready, at(r, SUB * NT, SUB * t))
                        nc.gpsimd.tensor_tensor(rstd[:, 0, :], rstd[:, 1, :], k.mhalf[:, :], ALU.pow).then_inc(rstd_ready, 1)

            @block.tensor
            def _(pe):
                pr.lead(pe, "pe")
                for s, n in ((att_turned, NT), (o_ready, 2 * NT), (x1_turned, NT), (gate_ready, NT), (comb_turned, NT),
                             (be_ready, 2 * NT), (exp_tile, SUB * NE * NT)):
                    pe.sem_inc(s, n)
                pe.wait_ge(pr.consts, pr.n_consts)
                pe.wait_ge(consts, 16 * (5 + C + SUB))

                def turn(src, then):
                    for c in range(C):
                        for s in range(SUB):
                            last = nc.tensor.transpose(ps[:, 6 + c, s * P:(s + 1) * P], src[:, s, c * P:(c + 1) * P], k.ident[:, :])
                    last.then_inc(then, 1)

                def out_projection(r, t):
                    pe.wait_ge(att_copied, at(r, NT, t + 1))
                    pe.wait_ge(pr.norm_read, at(r, 2 * NT, 2 * t))
                    if t == 0:
                        pe.wait_ge(comb_copied, at(r, NT, 0))
                    turn(att, att_turned)
                    pe.wait_ge(att_t_copied, at(r, 2 * NT, 2 * t + 2))
                    pe.wait_ge(pr.v_copied, at(r, 2 * NT, 2 * t))
                    if t == 0:
                        pe.wait_ge(be_added, at(r, 2 * NT, 0))
                    for b in range(2):
                        for s in range(2):
                            for c in range(C):
                                last = nc.tensor.matmul(ps[:, 4 + b, s * D:(s + 1) * D],
                                                        att_t[:, c, (2 * b + s) * P:(2 * b + s + 1) * P], wo[:, c, :],
                                                        start=c == 0, stop=c == C - 1)
                        last.then_inc(o_ready, 1)

                def turn_x1_and_project(r, t):
                    pe.wait_ge(x1_ready, at(r, SUB * NT, SUB * (t + 1)))
                    pe.wait_ge(comb_copied, at(r, NT, t))
                    turn(x1[:, t % 2, :, :], x1_turned)
                    pe.wait_ge(x1t_copied, at(r, 2 * NT, 2 * t + 2))
                    for s in range(SUB):
                        for c in range(C):
                            last = nc.tensor.matmul(ps[:, 6, s * E:(s + 1) * E], x1t[:, c, s * P:(s + 1) * P], wg[:, c, :],
                                                    start=c == 0, stop=c == C - 1)
                    last.then_inc(gate_ready, 1)
                    pe.wait_ge(exp_added, at(r, SUB * E * NT, SUB * E * t))
                    pr.pe_tiles(pe, r, t, x1t)
                    pe.wait_ge(o_added, at(r, 2 * NT, 2 * t + 2))
                    pe.wait_ge(be_added, at(r, 2 * NT, 2 * t))
                    pr.pe_v(pe, r, t, x1t)
                    pe.wait_ge(gate_step, at(r, GS * NT, GS * t + 1))
                    pr.pe_norms(pe, r, t)

                def experts(r, t):
                    pe.wait_ge(gate_step, at(r, GS * NT, GS * (t + 1)))
                    if t + 1 < NT:
                        pe.wait_ge(att_t_copied, at(r, 2 * NT, 2 * t + 4))
                    else:
                        pe.wait_ge(pr.norm_read, at(r, 2 * NT, 2 * t + 2))
                    for s in range(SUB):
                        last = nc.tensor.transpose(ps[0:E, 6, s * P:(s + 1) * P], comb[:, t % 2, s, :], k.ident[:, :])
                    last.then_inc(comb_turned, 1)
                    pe.wait_ge(comb_copied, at(r, NT, t + 1))
                    if t + 1 < NT:
                        pe.wait_ge(o_added, at(r, 2 * NT, 2 * t + 4))
                    else:
                        pe.wait_ge(pr.v_copied, at(r, 2 * NT, 2 * t + 2))
                    for b in range(2):
                        for s in range(2):
                            last = nc.tensor.matmul(ps[:, 4 + b, s * D:(s + 1) * D],
                                                    comb_t[:, (2 * b + s) * P:(2 * b + s + 1) * P], be[:, :],
                                                    start=True, stop=True)
                        last.then_inc(be_ready, 1)
                    pe.wait_ge(pr.qk_copied, at(r, 4 * NT, 4 * t + 4))
                    for s in range(SUB):
                        for e in range(NE):
                            n = s * NE + e
                            if n >= 4:
                                pe.wait_ge(exp_added, at(r, SUB * E * NT, SUB * E * t + 2 * (n - 3)))
                            for c in range(C):
                                last = nc.tensor.matmul(ps[:, n % 4, :], x1t_of[t % 2][:, c, s * P:(s + 1) * P],
                                                        we[:, c, 2 * e * D:2 * (e + 1) * D], start=c == 0, stop=c == C - 1)
                            last.then_inc(exp_tile, 1)

                x1t_of = [x1t, x1t]
                with rounds(k, mybir.EngineType.PE, B) as r:
                    out_projection(r, 0)
                    turn_x1_and_project(r, 0)
                    for t in range(NT):
                        if t + 1 < NT:
                            out_projection(r, t + 1)
                        experts(r, t)
                        if t + 1 < NT:
                            turn_x1_and_project(r, t + 1)

            @block.scalar
            def _(act):
                pr.lead(act, "act")
                for s, n in ((att_t_copied, 2 * NT), (x1t_copied, 2 * NT), (exp_ready, NT), (comb_copied, NT)):
                    act.sem_inc(s, n)
                act.wait_ge(pr.consts, pr.n_consts)

                def copy_turned(r, t, turned, dst, then):
                    act.wait_ge(turned, at(r, NT, t + 1))
                    for c in range(C):
                        nc.scalar.activation(dst[:, c, :], ps[:, 6 + c, :], ACT.Copy).then_inc(then, 1)

                def project_block(r, t):
                    copy_turned(r, t, x1_turned, x1t, x1t_copied)
                    act.wait_ge(gate_step, at(r, GS * NT, GS * t + 3))
                    nc.scalar.activation(expd[:, :, :], logit[:, :, :], ACT.Exp).then_inc(exp_ready, 1)
                    pr.act_tiles(act, r, t)

                def copy_comb(r, t):
                    act.wait_ge(comb_turned, at(r, NT, t + 1))
                    act.wait_ge(be_ready, at(r, 2 * NT, 2 * t))
                    nc.scalar.activation(comb_t[:, :], ps[0:E, 6, :], ACT.Copy).then_inc(comb_copied, 1)

                with rounds(k, mybir.EngineType.Activation, B) as r:
                    copy_turned(r, 0, att_turned, att_t, att_t_copied)
                    project_block(r, 0)
                    for t in range(NT):
                        if t + 1 < NT:
                            copy_turned(r, t + 1, att_turned, att_t, att_t_copied)
                        copy_comb(r, t)
                        if t + 1 < NT:
                            project_block(r, t + 1)
                    pr.act_root(act, r)

            @block.vector
            def _(dve):
                pr.lead(dve, "dve")
                for s, n in ((pr.v_copied, 2 * NT), (o_added, 2 * NT), (ln_step, 8 * NT), (x1_ready, SUB * NT),
                             (gate_step, GS * NT), (be_added, 2 * NT), (exp_added, SUB * E * NT)):
                    dve.sem_inc(s, n)
                nc.vector.memset(pr.v[:, :, :, DK:VW], 1.0).then_inc(pr.set, 1)
                dve.wait_ge(pr.set, 1)
                dve.wait_ge(consts, 16 * (5 + C + SUB))

                def layer_norm(r, t):
                    y = xr[:, t % 2, :, :]
                    dve.wait_ge(x_loaded[t % 2], at(r, 16 * half, 16 * (t // 2 + 1)))
                    for b in range(2):
                        dve.wait_ge(o_ready, at(r, 2 * NT, 2 * t + b + 1))
                        nc.vector.tensor_tensor(y[:, 2 * b:2 * b + 2, :], ps[:, 4 + b, :].rearrange("p (s d) -> p s d", s=2),
                                                y[:, 2 * b:2 * b + 2, :], ALU.add).then_inc(o_added, 1)
                    for s in range(SUB):
                        dve.wait_ge(o_added, at(r, 2 * NT, 2 * t + s // 2 + 1))
                        nc.vector.bn_stats(stats[:, s, :], y[:, s, :]).then_inc(ln_step, 1)
                    if t >= 0:
                        dve.wait_ge(rstd_ready, at(r, 2 * NT, 2 * t))
                    for s in range(SUB):
                        dve.wait_ge(ln_step, at(r, 8 * NT, 8 * t + s + 1))
                        carry(k)
                        nc.vector.bn_aggr(mv[:, s, :], stats[:, s, :]).then_inc(ln_step, 1)
                    dve.wait_ge(ln_step, at(r, 8 * NT, 8 * t + 8))
                    dve.wait_ge(rstd_ready, at(r, 2 * NT, 2 * t + 2))
                    dve.wait_ge(exp_added, at(r, SUB * E * NT, SUB * E * (t - 1)))
                    for s in range(SUB):
                        nc.vector.tensor_scalar(x1[:, t % 2, s, :], y[:, s, :], mv[:, s, 0:1], rstd[:, 0, s:s + 1],
                                                ALU.subtract, ALU.mult).then_inc(x1_ready, 1)

                def gating(r, t):
                    count = [0]

                    def step(ins):
                        count[0] += 1
                        ins.then_inc(gate_step, 1)
                        dve.wait_ge(gate_step, at(r, GS * NT, GS * t + count[0]))

                    wide = lambda x: x.unsqueeze(2).to_broadcast([P, SUB, E])
                    dve.wait_ge(gate_ready, at(r, NT, t + 1))
                    step(nc.vector.tensor_tensor(logit[:, :, :], ps[:, 6, 0:SUB * E].rearrange("p (s e) -> p s e", s=SUB),
                                                 bg[:, :, :], ALU.add))
                    step(nc.vector.tensor_reduce(small[:, :, 0], logit[:, :, :], AX.X, ALU.max))
                    step(nc.vector.tensor_tensor(logit[:, :, :], logit[:, :, :], wide(small[:, :, 0]), ALU.subtract))
                    dve.wait_ge(exp_ready, at(r, NT, t + 1))
                    step(nc.vector.tensor_reduce(small[:, :, 1], expd[:, :, :], AX.X, ALU.add))
                    step(nc.vector.reciprocal(small[:, :, 2], small[:, :, 1]))
                    step(nc.vector.tensor_tensor(gate[:, :, :], expd[:, :, :], wide(small[:, :, 2]), ALU.mult))
                    for s in range(SUB):
                        carry(k)
                        step(nc.vector.max(top[:, s, :], gate[:, s, :]))
                    for s in range(SUB):
                        carry(k)
                        step(nc.vector.max_index(topi[:, s, :], top[:, s, :], gate[:, s, :]))
                    step(nc.vector.tensor_copy(topf[:, :, :], topi[:, :, :]))
                    io = iota[:, :].unsqueeze(1).to_broadcast([P, SUB, E])
                    step(nc.vector.tensor_tensor(hot[:, :, :], io, wide(topf[:, :, 0]), ALU.is_equal))
                    step(nc.vector.tensor_tensor(logit[:, :, :], io, wide(topf[:, :, 1]), ALU.is_equal))
                    step(nc.vector.tensor_tensor(hot[:, :, :], hot[:, :, :], logit[:, :, :], ALU.add))
                    step(nc.vector.tensor_tensor(comb[:, t % 2, :, :], hot[:, :, :], gate[:, :, :], ALU.mult))
                    nc.vector.tensor_copy(small[:, :, 3], small[:, :, 2]).then_inc(gate_step, 1)
                    assert count[0] + 1 == GS, count

                def add_experts(r, t):
                    acc = x1[:, t % 2, :, :]
                    for b in range(2):
                        dve.wait_ge(be_ready, at(r, 2 * NT, 2 * t + b + 1))
                        nc.vector.tensor_tensor(acc[:, 2 * b:2 * b + 2, :], ps[:, 4 + b, :].rearrange("p (s d) -> p s d", s=2),
                                                acc[:, 2 * b:2 * b + 2, :], ALU.add).then_inc(be_added, 1)
                    for s in range(SUB):
                        dve.wait_ge(be_added, at(r, 2 * NT, 2 * t + s // 2 + 1))
                        for e in range(E):
                            n = s * E + e
                            dve.wait_ge(exp_tile, at(r, SUB * NE * NT, SUB * NE * t + n // 2 + 1))
                            if e:
                                dve.wait_ge(exp_added, at(r, SUB * E * NT, SUB * E * t + n))
                            dst = acc[:, s, :]
                            if e == E - 1:
                                dst = k.tok[:, bass.ds(r * NKB + t * SUB + s, 1), :].rearrange("p o d -> p (o d)")
                            nc.vector.scalar_tensor_tensor(dst, ps[:, (n // 2) % 4, (n % 2) * D:(n % 2 + 1) * D],
                                                           comb[:, t % 2, s, e:e + 1], acc[:, s, :], ALU.mult,
                                                           ALU.add).then_inc(exp_added, 1)

                def project_block(r, t):
                    gating(r, t)
                    pr.dve_split(dve, r, t)
                    pr.dve_v(dve, r, t, bv)
                    pr.dve_norms(dve, r, t)

                with rounds(k, mybir.EngineType.DVE, B) as r:
                    layer_norm(r, 0)
                    project_block(r, 0)
                    for t in range(NT):
                        if t + 1 < NT:
                            layer_norm(r, t + 1)
                        add_experts(r, t)
                        if t + 1 < NT:
                            project_block(r, t + 1)
                    pr.dve_shift(dve, r)
                pr.dve_flag(dve)


def norm_out(k):
    nc = k.nc
    with ExitStack() as ctx:
        stats = k.sb("stats_out", [P, SUB, 6], F32, ctx)
        mv = k.sb("mv_out", [P, SUB, 2], F32, ctx)
        var = k.sb("var_out", [P, SUB], F32, ctx)
        rstd = k.sb("rstd_out", [P, SUB], F32, ctx)
        ln_step = k.sem("out_ln_step")
        rstd_ready = k.sem("out_rstd_ready")
        normed = k.sem("out_normed")
        stored = k.sem("out_stored")
        with nc.Block() as block:

            @block.vector
            def _(dve):
                dve.sem_inc(ln_step, 8)
                dve.sem_inc(normed, SUB)
                with rounds(k, mybir.EngineType.DVE, N_BLOCKS) as r:
                    for s in range(SUB):
                        nc.vector.bn_stats(stats[:, s, :], k.tok[:, bass.ds(r * SUB + s, 1), :].rearrange("p o d -> p (o d)")).then_inc(ln_step, 1)
                    for s in range(SUB):
                        dve.wait_ge(ln_step, at(r, 8, s + 1))
                        carry(k)
                        nc.vector.bn_aggr(mv[:, s, :], stats[:, s, :]).then_inc(ln_step, 1)
                    dve.wait_ge(rstd_ready, at(r, 2, 2))
                    dve.wait_ge(ln_step, at(r, 8, 8))
                    for s in range(SUB):
                        row = k.tok[:, bass.ds(r * SUB + s, 1), :].rearrange("p o d -> p (o d)")
                        nc.vector.tensor_scalar(row, row, mv[:, s, 0:1], rstd[:, s:s + 1], ALU.subtract, ALU.mult).then_inc(normed, 1)
                    dve.wait_ge(normed, at(r, SUB, SUB))

            @block.gpsimd
            def _(pool):
                pool.sem_inc(rstd_ready, 2)
                with rounds(k, mybir.EngineType.Pool, N_BLOCKS) as r:
                    pool.wait_ge(ln_step, at(r, 8, 8))
                    nc.gpsimd.tensor_tensor(var[:, :], mv[:, :, 1], k.eps[:, :], ALU.add).then_inc(rstd_ready, 1)
                    pool.wait_ge(rstd_ready, at(r, 2, 1))
                    nc.gpsimd.tensor_tensor(rstd[:, :], var[:, :], k.mhalf[:, :], ALU.pow).then_inc(rstd_ready, 1)

            @block.sync
            def _(sp):
                out_f = k.out.rearrange("b (n p) d -> p (b n) d", p=P)
                with rounds(k, mybir.EngineType.SP, N_BLOCKS) as r:
                    alone(sp, k)
                    sp.wait_ge(normed, at(r, SUB, SUB))
                    sp.dma_start(out_f[:, bass.ds(r * SUB, SUB), :], k.tok[:, bass.ds(r * SUB, SUB), :]).then_inc(stored, 16)
                sp.wait_ge(stored, 16 * N_BLOCKS)


def program(nc, args, out):
    with ExitStack() as ctx:
        k = Build(nc, ctx, args, out)
        start(k)
        project(k)
        row_max(k, 1)
        attend(k, 1)
        middle(k)
        row_max(k, 2)
        attend(k, 2)
        norm_out(k)


def kernel(L0_attn_X, L0_attn_q_proj, L0_attn_k_proj, L0_attn_v_proj, L0_attn_o_proj, L0_ffn_W_qkv, L0_ffn_b_qkv,
           L0_ffn_W_gate, L0_ffn_b_gate, L0_ffn_W_experts, L0_ffn_b_experts):
    import concourse.bacc as _bacc
    import ml_dtypes
    from concourse.bass_utils import run_bass_kernel_spmd as _run

    lay = np.ascontiguousarray
    x = np.asarray(L0_attn_X)
    head_of = np.arange(P)[:, None] // DK == np.arange(32)[None, :]
    bf = ml_dtypes.bfloat16
    arrays = {
        "x": x,
        "xt": lay(np.swapaxes(x, 1, 2)),
        "wqk1": lay(np.concatenate([np.asarray(L0_attn_q_proj).T, np.asarray(L0_attn_k_proj).T], axis=1)),
        "wv1": lay(np.asarray(L0_attn_v_proj).T),
        "wo": lay(np.asarray(L0_attn_o_proj).T),
        "wqk2": lay(np.asarray(L0_ffn_W_qkv)[:, :2 * D]),
        "wv2": lay(np.asarray(L0_ffn_W_qkv)[:, 2 * D:]),
        "b_qkv": np.asarray(L0_ffn_b_qkv),
        "wg": np.asarray(L0_ffn_W_gate),
        "b_gate": np.asarray(L0_ffn_b_gate),
        "w_exp": np.asarray(L0_ffn_W_experts),
        "b_exp": np.asarray(L0_ffn_b_experts),
        "ident": np.eye(P, dtype=np.float32),
        "identb": np.eye(P, dtype=np.float32).astype(bf),
        "mask": np.where(np.arange(P)[:, None] > np.arange(P)[None, :], MASK, 0.0).astype(bf),
        "mask_wide": np.where(np.arange(QT)[None, None, :] > np.arange(P)[:, None, None] + P * np.arange(SUB)[None, :, None],
                              MASK, 0.0).astype(np.float32),
        "iota": np.tile(np.arange(E, dtype=np.float32), (P, 1)),
        "sums": (head_of * MARGIN).astype(bf),
    }
    nc = _bacc.Bacc("TRN2", target_bir_lowering=False, num_devices=1)
    args = {n: nc.dram_tensor(f"in_{n}", v.shape, mybir.dt.from_np(v.dtype), kind="ExternalInput").ap()
            for n, v in arrays.items()}
    out = nc.dram_tensor("out_0", (B, S, D), F32, kind="ExternalOutput").ap()
    program(nc, args, out)
    r = _run(nc, [{f"in_{n}": v for n, v in arrays.items()}], core_ids=[0])
    return r.results[0]["out_0"]
```

```python
from contextlib import ExitStack

import concourse.bass as bass
import numpy as np
from concourse import mybir

F32 = mybir.dt.float32
BF16 = mybir.dt.bfloat16
F32R = mybir.dt.float32r
I32 = mybir.dt.int32
U32 = mybir.dt.uint32
ALU = mybir.AluOpType
ACT = mybir.ActivationFunctionType
AX = mybir.AxisListType

P = 128
B, S, D = 4, 2048, 256
H, E = 16, 8
DK = D // H
G = 4
NG = H // G
QT = 512
NT = S // QT
NKB = S // P
SUB = QT // P
C = D // P
HM = P // DK
PARTS = 3
ROWS = 6 * DK
VW = DK + 1
SCALE = DK ** -0.5
EPS = 1e-5
UNDER = 16.0
SHIFT_MAX = (87.0 - 24.0 + UNDER) / 2 - UNDER
ROOT_MAX = 2.0 ** 100
MASK = -1e30
MARGIN = 1 + 1 / 64
NSC = 3
NPR = 8
N_BLOCKS = B * NT


def at(r, per, c):
    return (r + 1) * per + c


def before(u, n, ring):
    if u >= ring:
        return u - ring + 1
    last = max(v for v in range(n) if v % ring == u % ring)
    return last + 1 - n


def rounds(k, engine, n):
    return k.nc.Fori(0, n, engines=[engine], hint_back_edge=True)


def product(k, out, x, xs, w, ws, x_moves=False):
    terms = [(0, wp, c) for c in range(C) for wp in range(2)] + [(1, 0, c) for c in range(C)]
    for n, (xp, wp, c) in enumerate(terms):
        pair = (x[xp][:, c, xs], w[wp][:, c, ws])
        held, moving = pair[::-1] if x_moves else pair
        last = k.nc.tensor.matmul(out, held, moving, start=n == 0, stop=n == len(terms) - 1)
    return last


def alone(engine, k):
    engine.wait_ge(k.ident_loaded, 16)


def carry(k):
    k.carried += 1
    k.nc.vector.memset(k.unused[:, k.carried:k.carried + 1], 0.0)


class Build:

    def __init__(self, nc, ctx, args, out):
        self.nc, self.ctx, self.a, self.out = nc, ctx, args, out
        self.ps = ctx.enter_context(nc.psum_tensor("ps", [P, 8, QT], F32))
        self.tok = self.sb("tok", [P, B * NKB, D], F32)
        self.ident = self.sb("ident", [P, P], F32)
        self.eps = self.sb("eps", [P, SUB], F32)
        self.mhalf = self.sb("mhalf", [P, SUB], F32)
        self.unused, self.carried = self.sb("unused", [1, 192], F32), 0
        self.flag = self.sb("flag", [1, 2], I32)
        self.qs = nc.dram_tensor("q_parts", [B, H, PARTS * DK, S], BF16).ap()
        self.ks = nc.dram_tensor("k_parts", [B, H, PARTS * DK, S], BF16).ap()
        self.ms = nc.dram_tensor("minus_shift", [B, H, S], BF16).ap()
        self.vs = nc.dram_tensor("v_ones", [B, NG, NKB, P, G * VW], F32).ap()

    def sb(self, name, shape, dt, ctx=None):
        return (ctx or self.ctx).enter_context(self.nc.sbuf_tensor(name, shape, dt))

    def sem(self, name, ctx=None):
        return self.ctx.enter_context(self.nc.semaphore(name))


def start(k):
    nc, ps = k.nc, k.ps
    loaded = k.ident_loaded = k.sem("ident_loaded")
    zeroed = k.sem("psum_zeroed")
    with nc.Block() as block:

        @block.sync
        def _(sp):
            sp.dma_start(k.ident[:, :], k.a["ident"]).then_inc(loaded, 16)
            sp.wait_ge(loaded, 16)

        @block.vector
        def _(dve):
            for n in range(8):
                nc.vector.memset(ps[:, n, :], 0.0).then_inc(zeroed, 1)
            nc.vector.memset(k.eps[:, :], EPS).then_inc(zeroed, 1)
            nc.vector.memset(k.mhalf[:, :], -0.5).then_inc(zeroed, 1)
            nc.vector.memset(k.flag[:, :], 0).then_inc(zeroed, 1)
            dve.wait_ge(zeroed, 11)


class Weights:

    def __init__(self, k, ctx, layer):
        self.k, self.layer = k, layer
        two = lambda name, n: [k.sb(f"{name}{layer}_{part}", [P, C, n], F32R, ctx) for part in ("high", "low")]
        self.vn = D + (E if layer == 2 else 0)
        self.wqkv = two("wqkv", 2 * D + self.vn)
        self.wqk = [w[:, :, 0:2 * D] for w in self.wqkv]
        self.wv = [w[:, :, 2 * D:] for w in self.wqkv]
        if layer == 2:
            self.wo, self.we = two("wo", D), two("we", E * D)
        self.step = k.sem(f"weights_split_{layer}")

    def stage(self, ctx):
        self.raw = self.k.sb(f"raw{self.layer}", [P, 2, E * D // 2], F32, ctx)
        self.loaded = [self.k.sem(f"weights_loaded{p}_{self.layer}") for p in range(2)]

    def pieces(self):
        a = self.k.a
        wqkv, wo = (w.rearrange("(c p) n -> p c n", p=P) for w in (a["wqkv2"], a["wo"]))
        out = [(wqkv[:, c, :], self.wqkv, c, 0, 3 * D + E) for c in range(C)]
        out += [(wo[:, c, :], self.wo, c, 0, D) for c in range(C)]
        for c in range(C):
            for e in range(0, E, E // 2):
                out.append((a["w_exp"][e:e + E // 2, c * P:(c + 1) * P, :].rearrange("e p n -> p e n"),
                            self.we, c, e * D, E // 2 * D))
        return out

    def load(self, engine, n):
        src, _, _, _, width = self.pieces()[n]
        dst = self.raw[:, n % 2, 0:width]
        if len(src.shape) == 3:
            dst = dst.rearrange("p (e n) -> p e n", n=D)
        engine.dma_start(dst, src).then_inc(self.loaded[n % 2], 16)

    def prepare(self, pool):
        nc = self.k.nc
        for n in range(2):
            self.load(pool, n)
        for n, (_, parts, c, at_col, width) in enumerate(self.pieces()):
            raw = self.raw[:, n % 2, 0:width]
            high, low = (part[:, c, at_col:at_col + width] for part in parts)
            pool.wait_ge(self.loaded[n % 2], 16 * (n // 2 + 1))
            nc.gpsimd.tensor_copy(high, raw).then_inc(self.step, 1)
            pool.wait_ge(self.step, 2 * n + 1)
            nc.gpsimd.tensor_tensor(low, raw, high.bitcast(F32), ALU.subtract).then_inc(self.step, 1)
            pool.wait_ge(self.step, 2 * n + 2)
            if n + 2 < len(self.pieces()):
                self.load(pool, n + 2)


class Projection:

    def __init__(self, k, ctx, layer, weights):
        self.k, self.layer = k, layer
        self.wqk, self.wv, self.vn = weights.wqk, weights.wv, weights.vn
        sb = lambda name, shape, dt: k.sb(f"{name}{layer}", shape, dt, ctx)
        sem = lambda name: k.sem(f"{name}_{layer}")
        self.sums = sb("sums", [P, 32], BF16)
        self.bias = sb("bias", [P, 4], F32)
        self.qf = sb("qf", [P, 4, QT], F32)
        self.part = sb("part", [P, 4, PARTS, QT], BF16)
        self.rest = sb("rest", [P, 2, QT], F32)
        self.sq = sb("sq", [P, 4, QT], BF16)
        self.v = sb("v", [P, SUB, H, VW], F32)
        self.qn = sb("qn", [40, S], F32)
        self.kn = sb("kn", [40, NT], F32)
        self.kmax = sb("kmax", [40, 1], F32)
        self.mshift = sb("mshift", [40, S], BF16)
        self.least = sb("least", [40, B], F32)
        self.least_row = sb("least_row", [1, B * H], F32)
        self.least1 = sb("least1", [1, 1], F32)
        self.consts, self.n_consts = sem("projection_consts"), 32 if layer == 2 else 16
        self.set = sem("ones_set")
        self.qk_ready = sem("qk_ready")
        self.qk_copied = sem("qk_copied")
        self.part_ready = sem("part_ready")
        self.sq_ready = sem("sq_ready")
        self.split = sem("split")
        self.stored_part = [sem(f"stored_part{n}") for n in range(4)]
        self.v_ready = sem("v_ready")
        self.v_copied = sem("v_copied")
        self.stored_v = sem("stored_v")
        self.norm_ready = sem("norm_ready")
        self.norm_read = sem("norm_read")
        self.shift_step = sem("shift_step")
        self.root_ready = sem("root_ready")
        self.stored_shift = sem("stored_shift")

    def sp_consts(self, sp):
        k, l = self.k, self.layer
        a = k.a
        sp.dma_start(self.sums[:, :], a["sums"]).then_inc(self.consts, 16)
        if l == 2:
            with self.k.nc.allow_non_contiguous_dma(reason="a bias per partition"):
                sp.dma_start(self.bias[:, :], a["b_qkv"][0:2 * D].rearrange("(n p) -> p n", p=P)).then_inc(self.consts, 16)

    def pe_tiles(self, pe, r, t, xt):
        for n in range(4):
            pe.wait_ge(self.qk_copied, at(r, 4 * NT, 4 * (t - 1) + n + 1))
            if n == 2:
                pe.wait_ge(self.norm_read, at(r, 2 * NT, 2 * t))
            product(self.k, self.k.ps[:, n, :], xt, slice(0, QT), self.wqk, slice(n * P, (n + 1) * P),
                    x_moves=True).then_inc(self.qk_ready, 1)

    def pe_v(self, pe, r, t, xt):
        for s in range(SUB):
            pe.wait_ge(self.v_copied, at(r, SUB * NT, SUB * (t - 1) + s + 1))
            product(self.k, self.k.ps[:, 4 + s, 0:self.vn], xt, slice(s * P, (s + 1) * P), self.wv,
                    slice(0, self.vn)).then_inc(self.v_ready, 1)

    def pe_norms(self, pe, r, t):
        nc, ps = self.k.nc, self.k.ps
        pe.wait_ge(self.sq_ready, at(r, 4 * NT, 4 * t + 4))
        for n in range(4):
            row = 32 * (n % 2)
            last = nc.tensor.matmul(ps[row:row + 32, 2 + n // 2, :], self.sums[:, :],
                                    self.sq[:, n, :], start=True, stop=True)
        last.then_inc(self.norm_ready, 1)

    def act_tiles(self, act, r, t):
        nc, ps = self.k.nc, self.k.ps
        for n in range(4):
            qf = self.qf[:, n, :]
            act.wait_ge(self.qk_ready, at(r, 4 * NT, 4 * t + n + 1))
            act.wait_ge(self.split, at(r, 12 * NT, 12 * (t - 1) + 3 * n + 1))
            bias = self.bias[:, n:n + 1] if self.layer == 2 else 0.0
            nc.scalar.activation(qf, ps[:, n, :], ACT.Identity, bias=bias).then_inc(self.qk_copied, 1)
            act.wait_ge(self.qk_copied, at(r, 4 * NT, 4 * t + n + 1))
            act.wait_ge(self.stored_part[n], at(r, 48 * NT, 48 * t))
            nc.scalar.activation(self.part[:, n, 0, :], qf, ACT.Copy).then_inc(self.part_ready, 1)
            if n == 0:
                act.wait_ge(self.norm_ready, at(r, NT, t))
            nc.scalar.activation(self.sq[:, n, :], qf, ACT.Square).then_inc(self.sq_ready, 1)

    def act_v(self, act, r, t):
        nc, ps = self.k.nc, self.k.ps
        for s in range(SUB):
            act.wait_ge(self.v_ready, at(r, SUB * NT, SUB * t + s + 1))
            if s == 0:
                act.wait_ge(self.stored_v, at(r, 64 * NT, 64 * t))
            nc.scalar.activation(self.v[:, s, :, 0:DK], ps[:, 4 + s, 0:D].rearrange("p (h e) -> p h e", e=DK),
                                 ACT.Copy).then_inc(self.v_copied, 1)

    def dve_v(self, dve, r, t, bias):
        nc, ps = self.k.nc, self.k.ps
        for s in range(SUB):
            dve.wait_ge(self.v_ready, at(r, SUB * NT, SUB * t + s + 1))
            if s == 0:
                dve.wait_ge(self.stored_v, at(r, 64 * NT, 64 * t))
            nc.vector.tensor_tensor(self.v[:, s, :, 0:DK], ps[:, 4 + s, 0:D].rearrange("p (h e) -> p h e", e=DK),
                                    bias[:, :].rearrange("p (h e) -> p h e", e=DK), ALU.add).then_inc(self.v_copied, 1)

    def dve_split(self, dve, r, t):
        nc = self.k.nc
        for n in range(4):
            rest = self.rest[:, n % 2, :]
            step = lambda c: at(r, 12 * NT, 12 * t + 3 * n + c)
            dve.wait_ge(self.part_ready, at(r, 4 * NT, 4 * t + n + 1))
            dve.wait_ge(self.split, step(-3))
            nc.vector.tensor_tensor(rest, self.qf[:, n, :], self.part[:, n, 0, :], ALU.subtract).then_inc(self.split, 1)
            dve.wait_ge(self.split, step(1))
            nc.vector.tensor_copy(self.part[:, n, 1, :], rest).then_inc(self.split, 1)
            dve.wait_ge(self.split, step(2))
            nc.vector.tensor_tensor(self.part[:, n, 2, :], rest, self.part[:, n, 1, :], ALU.subtract).then_inc(self.split, 1)

    def dve_norms(self, dve, r, t):
        nc, ps = self.k.nc, self.k.ps
        dve.wait_ge(self.norm_ready, at(r, NT, t + 1))
        if t == 0:
            dve.wait_ge(self.shift_step, at(r, 4, 0))
        nc.vector.tensor_copy(self.qn[:, t * QT:(t + 1) * QT], ps[0:40, 2, :]).then_inc(self.norm_read, 1)
        nc.vector.tensor_reduce(self.kn[:, t:t + 1], ps[0:40, 3, :], AX.X, ALU.max).then_inc(self.norm_read, 1)
        if t == NT - 1:
            dve.wait_ge(self.norm_read, at(r, 2 * NT, 2 * NT))
            nc.vector.tensor_reduce(self.kmax[:, :], self.kn[:, :], AX.X, ALU.max).then_inc(self.shift_step, 1)
            dve.wait_ge(self.shift_step, at(r, 4, 1))
            nc.vector.tensor_scalar(self.qn[:, :], self.qn[:, :], self.kmax[:, 0:1], ROOT_MAX, ALU.mult,
                                    ALU.min).then_inc(self.shift_step, 1)

    def act_root(self, act, r):
        act.wait_ge(self.shift_step, at(r, 4, 2))
        self.k.nc.scalar.activation(self.qn[:, :], self.qn[:, :], ACT.Sqrt).then_inc(self.root_ready, 1)

    def dve_shift(self, dve, r):
        nc = self.k.nc
        dve.wait_ge(self.root_ready, at(r, 1, 1))
        dve.wait_ge(self.stored_shift, at(r, 32, 0))
        nc.vector.tensor_scalar(self.mshift[:, :], self.qn[:, :], -1.0, UNDER / SCALE, ALU.mult,
                                ALU.add).then_inc(self.shift_step, 1)
        dve.wait_ge(self.shift_step, at(r, 4, 3))
        nc.vector.tensor_reduce(self.least[:, bass.ds(r, 1)], self.mshift[:, :], AX.X, ALU.min).then_inc(self.shift_step, 1)

    def sp_store(self, sp, r, t):
        k = self.k
        for s in range(SUB):
            alone(sp, k)
            sp.wait_ge(self.v_copied, at(r, SUB * NT, SUB * t + s + 1))
            to = k.vs[bass.ds(r, 1), :, t * SUB + s, :, :].rearrange("b g p e -> p (b g) e")
            sp.dma_start(to, self.v[:, s, :, :].rearrange("p (g j) e -> p g (j e)", g=NG)).then_inc(self.stored_v, 16)
        for n in range(4):
            dst = (k.qs, k.ks)[n // 2]
            alone(sp, k)
            sp.wait_ge(self.split, at(r, 12 * NT, 12 * t + 3 * n + 3))
            for part in range(PARTS):
                to = dst[bass.ds(r, 1), HM * (n % 2):HM * (n % 2) + HM, part * DK:(part + 1) * DK, t * QT:(t + 1) * QT]
                sp.dma_start(to.rearrange("b h i s -> (b h) i s"), self.part[:, n, part, :]).then_inc(self.stored_part[n], 16)

    def sp_store_shift(self, sp, r):
        k = self.k
        alone(sp, k)
        sp.wait_ge(self.shift_step, at(r, 4, 3))
        for m in range(2):
            to = k.ms[bass.ds(r, 1), m * HM:(m + 1) * HM, :].rearrange("b h s -> (b h) s")
            sp.dma_start(to, self.mshift[32 * m:32 * m + HM, :]).then_inc(self.stored_shift, 16)

    def lead(self, engine, which):
        per = {"pe": ((self.qk_ready, 4 * NT), (self.v_ready, SUB * NT), (self.norm_ready, NT)),
               "act": ((self.root_ready, 1), (self.qk_copied, 4 * NT), (self.part_ready, 4 * NT), (self.sq_ready, 4 * NT)),
               "dve": ((self.split, 12 * NT), (self.norm_read, 2 * NT), (self.shift_step, 4)),
               "sp": tuple((x, 48 * NT) for x in self.stored_part) + ((self.stored_v, 64 * NT), (self.stored_shift, 32))}
        for s, n in per[which]:
            engine.sem_inc(s, n)

    def sp_end(self, sp):
        for x in self.stored_part:
            sp.wait_ge(x, at(B - 1, 48 * NT, 48 * NT))
        sp.wait_ge(self.stored_v, at(B - 1, 64 * NT, 64 * NT))
        sp.wait_ge(self.stored_shift, at(B - 1, 32, 32))
        sp.wait_ge(self.shift_step, at(B - 1, 4, 4))
        gathered = self.gathered = self.k.sem(f"least_gathered_{self.layer}")
        with self.k.nc.allow_non_contiguous_dma(reason="one number per head and batch"):
            for m in range(2):
                sp.dma_start(self.least_row[0:1, m * B * HM:(m + 1) * B * HM],
                             self.least[32 * m:32 * m + HM, :]).then_inc(gathered, 16)

    def dve_flag(self, dve):
        nc = self.k.nc
        step = self.k.sem(f"flag_step_{self.layer}")
        dve.wait_ge(self.gathered, 32)
        nc.vector.tensor_reduce(self.least1[:, :], self.least_row[:, :], AX.X, ALU.min).then_inc(step, 1)
        dve.wait_ge(step, 1)
        nc.vector.tensor_scalar(self.k.flag[:, self.layer - 1:self.layer], self.least1[:, :], -SHIFT_MAX / SCALE, None,
                                ALU.is_lt).then_inc(step, 1)
        dve.wait_ge(step, 2)


def project(k):
    nc = k.nc
    with ExitStack() as ctx:
        weights = Weights(k, ctx, 1)
        pr = Projection(k, ctx, 1, weights)
        raw_w = k.sb("wqkv1", [P, C, 3 * D], F32, ctx)
        raw_x = k.sb("xt_raw", [P, NT, C, QT], F32, ctx)
        xt_low = k.sb("xt_low", [P, NT, C, QT], F32R, ctx)
        xt_high = k.sb("xt_high", [P, NT, C, QT], F32R, ctx)
        unused = k.sb("unused_sums", [P, NT, SUB], F32, ctx)
        w_loaded = k.sem("wqkv1_loaded")
        x_loaded = [k.sem(f"x_loaded{t}") for t in range(NT)]
        x_split = k.sem("x_split")
        with nc.Block() as block:

            @block.sync
            def _(sp):
                def load_x(r, t):
                    src = k.a["xt"][bass.ds(r + t // NT, 1), :, t % NT * QT:(t % NT + 1) * QT]
                    sp.dma_start(raw_x[:, t % NT, :, :], src.rearrange("b (c p) s -> p (b c) s", p=P)).then_inc(x_loaded[t % NT], 16)

                sp.dma_start(raw_w[:, :, :], k.a["wqkv1"].rearrange("(c p) n -> p c n", p=P)).then_inc(w_loaded, 16)
                for s in x_loaded:
                    sp.sem_inc(s, 16)
                for t in range(NT - 1):
                    load_x(0, t)
                pr.sp_consts(sp)
                pr.lead(sp, "sp")

                def batch(r, last):
                    for t in range(NT):
                        if not last or t == 0:
                            alone(sp, k)
                            sp.wait_ge(x_split, at(r, 2 * NT, 2 * t))
                            load_x(r, t + NT - 1)
                        pr.sp_store(sp, r, t)
                    pr.sp_store_shift(sp, r)

                with rounds(k, mybir.EngineType.SP, B - 1) as r:
                    batch(r, False)
                batch(B - 1, True)
                pr.sp_end(sp)

            @block.gpsimd
            def _(pool):
                pool.sem_inc(x_split, 2 * NT)
                with rounds(k, mybir.EngineType.Pool, B) as r:
                    for t in range(NT):
                        raw, high, low = raw_x[:, t, :, :], xt_high[:, t, :, :], xt_low[:, t, :, :]
                        pool.wait_ge(x_loaded[t], at(r, 16, 16))
                        pool.wait_ge(pr.qk_ready, at(r, 4 * NT, 4 * (t + 1 - NT)))
                        nc.gpsimd.tensor_tensor(unused[:, t, :], k.eps[:, :], k.eps[:, :], ALU.add)
                        nc.gpsimd.tensor_copy(high, raw).then_inc(x_split, 1)
                        pool.wait_ge(x_split, at(r, 2 * NT, 2 * t + 1))
                        nc.gpsimd.tensor_tensor(low, raw, high.bitcast(F32), ALU.subtract).then_inc(x_split, 1)

            @block.tensor
            def _(pe):
                pr.lead(pe, "pe")
                pe.wait_ge(pr.consts, pr.n_consts)
                pe.wait_ge(weights.step, 2)

                def values(r, t):
                    pe.wait_ge(x_split, at(r, 2 * NT, 2 * t + 2))
                    pr.pe_v(pe, r, t, (xt_high[:, t % NT, :, :], xt_low[:, t % NT, :, :]))

                def batch(r, last):
                    for t in range(NT):
                        pr.pe_tiles(pe, r, t, (xt_high[:, t, :, :], xt_low[:, t, :, :]))
                        if not last or t + 1 < NT:
                            values(r, t + 1)
                        pr.pe_norms(pe, r, t)

                values(0, 0)
                with rounds(k, mybir.EngineType.PE, B - 1) as r:
                    batch(r, False)
                batch(B - 1, True)

            @block.scalar
            def _(act):
                pr.lead(act, "act")
                act.sem_inc(pr.v_copied, SUB * NT)
                act.wait_ge(w_loaded, 16)
                nc.scalar.activation(weights.wqkv[0][:, :, :], raw_w[:, :, :], ACT.Copy).then_inc(weights.step, 1)
                act.wait_ge(pr.set, 1)

                def batch(r, last):
                    for t in range(NT):
                        pr.act_tiles(act, r, t)
                        if not last or t + 1 < NT:
                            pr.act_v(act, r, t + 1)
                    pr.act_root(act, r)

                pr.act_v(act, 0, 0)
                with rounds(k, mybir.EngineType.Activation, B - 1) as r:
                    batch(r, False)
                batch(B - 1, True)

            @block.vector
            def _(dve):
                nc.vector.memset(pr.v[:, :, :, DK:VW], 1.0).then_inc(pr.set, 1)
                pr.lead(dve, "dve")
                dve.wait_ge(weights.step, 1)
                nc.vector.tensor_tensor(weights.wqkv[1][:, :, :], raw_w[:, :, :], weights.wqkv[0][:, :, :].bitcast(F32),
                                        ALU.subtract).then_inc(weights.step, 1)
                with rounds(k, mybir.EngineType.DVE, B) as r:
                    for t in range(NT):
                        pr.dve_split(dve, r, t)
                        pr.dve_norms(dve, r, t)
                    pr.dve_shift(dve, r)
                pr.dve_flag(dve)


def row_max(k, layer):
    nc, ps = k.nc, k.ps
    causal = layer == 1
    R = B * H
    NQ = S // P
    chunks = lambda n: n // SUB + 1 if causal else NT
    with ExitStack() as ctx:
        sb = lambda name, shape, dt: k.sb(f"max_{name}{layer}", shape, dt, ctx)
        sem = lambda name: k.sem(f"max_{name}_{layer}")
        qst = sb("q", [ROWS, S], BF16)
        kst = sb("k", [ROWS, S], BF16)
        mask = sb("mask", [P, SUB, QT], F32)
        masked = sb("masked", [P, 2, QT], F32)
        part = sb("part", [P, NQ, NT], F32)
        biggest = sb("biggest", [P, NQ], F32)
        row = sb("row", [NQ, P], BF16)
        loaded, masks = sem("loaded"), sem("mask_loaded")
        cleared = sem("cleared")
        ready = sem("ready")
        read = sem("read")
        step = sem("step")
        turned = sem("turned")
        stored = sem("stored")
        on_mask = sem("on_mask")
        ND = 9
        qs_f = k.qs.rearrange("b h i s -> (b h) i s")
        ks_f = k.ks.rearrange("b h i s -> (b h) i s")
        ms_f = k.ms.rearrange("b h (n p) -> (b h) n p", p=P)

        def taken(engine):
            return engine.value_load(k.flag[0:1, layer - 1:layer], min_val=0, max_val=1)

        with nc.Block() as block:

            @block.sync
            def _(sp):
                with sp.If(taken(sp) > 0):
                    sp.dma_start(mask[:, :, :], k.a["mask_wide"]).then_inc(masks, 16)
                    sp.sem_inc(loaded, 16 * ND)
                    sp.sem_inc(stored, 16)
                    with rounds(k, mybir.EngineType.SP, R) as r:
                        alone(sp, k)
                        sp.wait_ge(read, at(r, NQ, 0))
                        at_row = 0
                        for n in (3, 2, 1):
                            src = qs_f[bass.ds(r, 1), 0:n * DK, :].rearrange("h i s -> (h i) s")
                            sp.dma_start(qst[at_row:at_row + n * DK, :], src).then_inc(loaded, 16)
                            part_k = 3 - n
                            for _ in range(n):
                                src = ks_f[bass.ds(r, 1), part_k * DK:(part_k + 1) * DK, :].rearrange("h i s -> (h i) s")
                                sp.dma_start(kst[at_row:at_row + DK, :], src).then_inc(loaded, 16)
                                at_row += DK
                        alone(sp, k)
                        sp.wait_ge(step, at(r, 2, 2))
                        sp.dma_start(ms_f[bass.ds(r, 1), :, :].rearrange("h n p -> (h n) p"), row[:, :]).then_inc(stored, 16)
                    sp.wait_ge(stored, 16 * (R + 1))

            @block.tensor
            def _(pe):
                with pe.If(taken(pe) > 0):
                    pe.sem_inc(ready, NQ)
                    pe.sem_inc(turned, 1)
                    with rounds(k, mybir.EngineType.PE, R) as r:
                        pe.wait_ge(loaded, at(r, 16 * ND, 16 * ND))
                        for n in range(NQ):
                            pe.wait_ge(read, at(r, NQ, n - 1))
                            if n == 0:
                                pe.wait_ge(step, at(r, 2, 0))
                            for c in range(chunks(n)):
                                last = nc.tensor.matmul(ps[:, 4 * (n % 2) + c, :], qst[:, n * P:(n + 1) * P],
                                                        kst[:, c * QT:(c + 1) * QT], start=True, stop=True)
                            last.then_inc(ready, 1)
                        pe.wait_ge(step, at(r, 2, 1))
                        nc.tensor.transpose(ps[0:NQ, 0, 0:P], biggest[:, :], k.ident[:, :]).then_inc(turned, 1)

            @block.vector
            def _(dve):
                with dve.If(taken(dve) > 0):
                    nc.vector.memset(part[:, :, :], -3e38).then_inc(cleared, 1)
                    dve.sem_inc(read, NQ)
                    dve.sem_inc(step, 2)
                    dve.sem_inc(on_mask, NQ)
                    dve.wait_ge(cleared, 1)
                    dve.wait_ge(masks, 16)
                    with rounds(k, mybir.EngineType.DVE, R) as r:
                        for n in range(NQ):
                            full = chunks(n) - (1 if causal else 0)
                            dve.wait_ge(ready, at(r, NQ, n + 1))
                            if n == 0:
                                dve.wait_ge(step, at(r, 2, 0))
                            bank = 4 * (n % 2)
                            if causal:
                                dve.wait_ge(read, at(r, NQ, n - 1))
                                nc.vector.tensor_tensor(masked[:, n % 2, :], ps[:, bank + full, :], mask[:, n % SUB, :],
                                                        ALU.add).then_inc(on_mask, 1)
                            if full:
                                last = nc.vector.tensor_reduce(part[:, n, 0:full], ps[:, bank:bank + full, :], AX.X, ALU.max)
                            if causal:
                                dve.wait_ge(on_mask, at(r, NQ, n + 1))
                                last = nc.vector.tensor_reduce(part[:, n, full:full + 1], masked[:, n % 2, :], AX.X, ALU.max)
                            last.then_inc(read, 1)
                        dve.wait_ge(read, at(r, NQ, NQ))
                        dve.wait_ge(turned, at(r, 1, 0))
                        nc.vector.tensor_reduce(biggest[:, :], part[:, :, :], AX.X, ALU.max).then_inc(step, 1)
                        dve.wait_ge(turned, at(r, 1, 1))
                        dve.wait_ge(stored, at(r, 16, 0))
                        nc.vector.tensor_scalar(row[:, :], ps[0:NQ, 0, 0:P], -1.0, None, ALU.mult).then_inc(step, 1)
                    dve.wait_ge(step, at(R - 1, 2, 2))


def attend(k, layer, weights=None):
    nc, ps = k.nc, k.ps
    causal = layer == 1
    quads = [(t, kb) for t in range(NT) for kb in range((t + 1) * SUB if causal else NKB)]
    NQ = len(quads)
    NH = 2 * NQ
    last_quad = [max(n for n, (t, _) in enumerate(quads) if t == u) for u in range(NT)]
    last_of_chunk = [max(n for n, (_, kb) in enumerate(quads) if kb // SUB == c) for c in range(NT)]
    R = B * NG
    off = lambda t, kb: max(0, kb - SUB * t) * P if causal else 0
    with ExitStack() as ctx:
        sb = lambda name, shape, dt: k.sb(f"{name}{layer}", shape, dt, ctx)
        sem = lambda name: k.sem(f"{name}_{layer}")
        if weights:
            weights.stage(ctx)
        qst = sb("q_stack", [ROWS + 1, G, S], BF16)
        kst = sb("k_stack", [ROWS + 1, G, S], BF16)
        vt = sb("v_keys", [P, NKB, G, VW], F32)
        prob = sb("prob", [P, NPR, 2, QT], F32)
        o_sb = sb("o_sb", [P, 2, QT], F32)
        rs = sb("rs", [P, 2, SUB, G], F32)
        o_n = sb("o_n", [P, 2, SUB, G, DK], F32)
        mask = sb("mask", [P, P], F32)
        warm = sb("warm", [P, 1], F32)
        warmed = sem("warmed")
        consts = sem("mask_loaded")
        ones_set = sem("k_ones_set")
        q_loaded = [sem(f"q_loaded{t}") for t in range(NT)]
        kv_loaded = [sem(f"kv_loaded{c}") for c in range(NT)]
        scores_ready = sem("scores_ready")
        probs_ready = sem("probs_ready")
        masked = sem("masked")
        pv_done = sem("pv_done")
        o_copied = sem("o_copied")
        o_turned = sem("o_turned")
        o_read = sem("o_read")
        if layer == 2:
            stats = sb("stats_out", [P, SUB, 6], F32)
            mv = sb("mv_out", [P, SUB, 2], F32)
            var = sb("var_out", [P, SUB], F32)
            rstd = sb("rstd_out", [P, SUB], F32)
            ln_step = sem("out_ln_step")
            rstd_ready = sem("out_rstd_ready")
            normed = sem("out_normed")
            stored = sem("out_stored")

        def load_q(sp, r, t):
            for row, n in ((0, 3), (3 * DK, 2), (5 * DK, 1)):
                src = qs_f[bass.ds(r * G, G), 0:n * DK, t * QT:(t + 1) * QT].rearrange("h i s -> i h s")
                sp.dma_start(qst[row:row + n * DK, :, t * QT:(t + 1) * QT], src).then_inc(q_loaded[t], 16)
            src = ms_f[bass.ds(r * G, G), t * QT:(t + 1) * QT].rearrange("(o h) s -> o h s", o=1)
            sp.dma_start(qst[ROWS:ROWS + 1, :, t * QT:(t + 1) * QT], src).then_inc(q_loaded[t], 16)

        def load_kv(sp, r, c):
            row = 0
            for part, n in ((0, 3), (1, 2), (2, 1)):
                for _ in range(n):
                    src = ks_f[bass.ds(r * G, G), part * DK:(part + 1) * DK, c * QT:(c + 1) * QT].rearrange("h i s -> i h s")
                    sp.dma_start(kst[row:row + DK, :, c * QT:(c + 1) * QT], src).then_inc(kv_loaded[c], 16)
                    row += DK
            src = vs_f[bass.ds(r, 1), c * SUB:(c + 1) * SUB, :, :].rearrange("b n p e -> p (b n) e")
            sp.dma_start(vt[:, c * SUB:(c + 1) * SUB, :, :].rearrange("p n j e -> p n (j e)"), src).then_inc(kv_loaded[c], 16)

        qs_f = k.qs.rearrange("b h i s -> (b h) i s")
        ks_f = k.ks.rearrange("b h i s -> (b h) i s")
        ms_f = k.ms.rearrange("b h s -> (b h) s")
        vs_f = k.vs.rearrange("b g n p e -> (b g) n p e")
        NQD, NKD = 4, 7
        OSTEPS = 3 if layer == 2 else 2

        with nc.Block() as block:

            @block.sync
            def _(sp):
                if causal:
                    sp.dma_start(mask[:, :], k.a["mask"]).then_inc(consts, 16)
                for s in q_loaded:
                    sp.sem_inc(s, 16 * NQD)
                for s in kv_loaded:
                    sp.sem_inc(s, 16 * NKD)
                for t in range(NT):
                    load_kv(sp, 0, t)
                    load_q(sp, 0, t)
                with rounds(k, mybir.EngineType.SP, R - 1) as last:
                    r = last + 1
                    for t in range(NT):
                        if t == NT - 1:
                            for c in range(NT):
                                alone(sp, k)
                                sp.wait_ge(pv_done, at(last, NQ, last_of_chunk[c] + 1))
                                load_kv(sp, r, c)
                        alone(sp, k)
                        sp.wait_ge(pv_done, at(last, NQ, last_quad[t] + 1))
                        load_q(sp, r, t)

            if weights:
                @block.gpsimd
                def _(pool):
                    weights.prepare(pool)
                    pool.wait_ge(weights.step, 2 * len(weights.pieces()))

            if layer == 2:
                @block.gpsimd
                def _(pool):
                    pool.sem_inc(rstd_ready, 2 * NT)
                    out_f = k.out.rearrange("b (n p) d -> p (b n) d", p=P)
                    with rounds(k, mybir.EngineType.Pool, B) as b:
                        for t in range(NT):
                            pool.wait_ge(ln_step, at(b, 8 * NT, 8 * t + 8))
                            nc.gpsimd.tensor_tensor(var[:, :], mv[:, :, 1], k.eps[:, :], ALU.add).then_inc(rstd_ready, 1)
                            pool.wait_ge(rstd_ready, at(b, 2 * NT, 2 * t + 1))
                            nc.gpsimd.tensor_tensor(rstd[:, :], var[:, :], k.mhalf[:, :], ALU.pow).then_inc(rstd_ready, 1)
                            pool.wait_ge(normed, at(b, SUB * NT, SUB * (t + 1)))
                            rows = bass.ds(b * NKB + t * SUB, SUB)
                            pool.dma_start(out_f[:, rows, :], k.tok[:, rows, :]).then_inc(stored, 16)
                    pool.wait_ge(stored, 16 * N_BLOCKS)

            @block.tensor
            def _(pe):
                pe.sem_inc(scores_ready, NH)
                pe.sem_inc(pv_done, NQ)
                pe.sem_inc(o_turned, NT)
                pe.wait_ge(ones_set, 1)

                def scores(r, u):
                    n, half = u // 2, u % 2
                    t, kb = quads[n]
                    w0 = off(t, kb)
                    if kb == 0 and half == 0:
                        pe.wait_ge(q_loaded[t], at(r, 16 * NQD, 16 * NQD))
                    if t == (kb // SUB if causal else 0) and kb % SUB == 0 and half == 0:
                        pe.wait_ge(kv_loaded[kb // SUB], at(r, 16 * NKD, 16 * NKD))
                    pe.wait_ge(probs_ready, at(r, NH, before(u, NH, NSC)))
                    for j in (2 * half, 2 * half + 1):
                        bank = 2 * (u % NSC) + j % 2
                        last = nc.tensor.matmul(ps[:, bank, w0:QT], kst[:, j, kb * P:(kb + 1) * P],
                                                qst[:, j, t * QT + w0:(t + 1) * QT], start=True, stop=True)
                    last.then_inc(scores_ready, 1)

                def values(r, n):
                    t, kb = quads[n]
                    w0 = off(t, kb)
                    if kb == 0:
                        pe.wait_ge(o_read, at(r, OSTEPS * NT, OSTEPS * (t - 1)))
                    pe.wait_ge(probs_ready, at(r, NH, 2 * n + 2))
                    if causal and kb >= SUB * t:
                        pe.wait_ge(masked, at(r, 2 * NKB, 2 * kb + 2))
                    for j in range(G):
                        last = nc.tensor.matmul(ps[32 * j:32 * j + VW, 6 + t % 2, w0:QT], vt[:, kb, j, :],
                                                prob[:, (2 * n + j // 2) % NPR, j % 2, w0:QT],
                                                start=kb == 0, stop=n == last_quad[t])
                    last.then_inc(pv_done, 1)

                def turn(r, t):
                    pe.wait_ge(o_copied, at(r, NT, t + 1))
                    for s in range(SUB):
                        last = nc.tensor.transpose(ps[:, 6 + t % 2, s * P:(s + 1) * P], o_sb[:, t % 2, s * P:(s + 1) * P],
                                                   k.ident[:, :])
                    last.then_inc(o_turned, 1)

                def ahead(r, u, final):
                    if u < NH:
                        scores(r, u)
                    elif not final:
                        scores(r + 1, u - NH)

                def round_of(r, final):
                    for n in range(NQ):
                        ahead(r, 2 * n + NSC, final)
                        if n + 1 < NQ:
                            ahead(r, 2 * n + NSC + 1, final)
                        values(r, n)
                        t, kb = quads[n]
                        if t and kb == 1:
                            turn(r, t - 1)
                    ahead(r, NH + NSC - 1, final)
                    turn(r, NT - 1)

                for u in range(NSC):
                    scores(0, u)
                with rounds(k, mybir.EngineType.PE, R - 1) as r:
                    round_of(r, False)
                round_of(R - 1, True)

            @block.scalar
            def _(act):
                act.sem_inc(probs_ready, NH)
                nc.scalar.activation(warm[:, :], k.eps[:, 0:1], ACT.Exp).then_inc(warmed, 1)
                act.wait_ge(warmed, 1)
                with rounds(k, mybir.EngineType.Activation, R) as r:
                    for n, half in ((n, half) for n in range(NQ) for half in range(2)):
                        t, kb = quads[n]
                        w0 = off(t, kb)
                        u = 2 * n + half
                        act.wait_ge(pv_done, at(r, NQ, (before(u, NH, NPR) + 1) // 2))
                        act.wait_ge(scores_ready, at(r, NH, u + 1))
                        sc = 2 * (u % NSC)
                        nc.scalar.activation(prob[:, u % NPR, :, w0:QT], ps[:, sc:sc + 2, w0:QT],
                                             ACT.Exp, scale=SCALE).then_inc(probs_ready, 1)

            @block.vector
            def _(dve):
                nc.vector.memset(kst[ROWS:ROWS + 1, :, :], 1.0).then_inc(ones_set, 1)
                dve.sem_inc(o_copied, NT)
                dve.sem_inc(o_read, OSTEPS * NT)

                def mask_diagonal(r, t):
                    for kb in range(SUB * t, SUB * (t + 1)):
                        for half in range(2):
                            u = 2 * quads.index((t, kb)) + half
                            dve.wait_ge(probs_ready, at(r, NH, u + 1))
                            part = prob[:, u % NPR, :, off(t, kb):off(t, kb) + P]
                            nc.vector.tensor_tensor(part, part, mask[:, :].unsqueeze(1).to_broadcast([P, 2, P]),
                                                    ALU.min).then_inc(masked, 1)

                def normalise(r, b, g, t):
                    dve.wait_ge(o_turned, at(r, NT, t + 1))
                    o = ps[:, 6 + t % 2, :].rearrange("p (s j e) -> p s j e", s=SUB, j=G)
                    step = lambda c: at(r, OSTEPS * NT, OSTEPS * t + c)
                    nc.vector.reciprocal(rs[:, t % 2, :, :], o[:, :, :, DK]).then_inc(o_read, 1)
                    dve.wait_ge(o_read, step(1))
                    to = k.tok[:, bass.ds(b * NKB + t * SUB, SUB), bass.ds(g * G * DK, G * DK)]
                    dst = to.rearrange("p s (j e) -> p s j e", j=G) if layer == 1 else o_n[:, t % 2, :, :, :]
                    nc.vector.tensor_tensor(dst, o[:, :, :, 0:DK],
                                            rs[:, t % 2, :, :].unsqueeze(3).to_broadcast([P, SUB, G, DK]),
                                            ALU.mult).then_inc(o_read, 1)
                    if layer == 2:
                        dve.wait_ge(o_read, step(2))
                        nc.vector.tensor_tensor(to, o_n[:, t % 2, :, :, :].rearrange("p s j e -> p s (j e)"), to,
                                                ALU.add).then_inc(o_read, 1)

                def last_norm(r, b, t):
                    row = lambda s: k.tok[:, bass.ds(b * NKB + t * SUB + s, 1), :].rearrange("p o d -> p (o d)")
                    dve.wait_ge(o_read, at(r, OSTEPS * NT, OSTEPS * (t + 1)))
                    for s in range(SUB):
                        nc.vector.bn_stats(stats[:, s, :], row(s)).then_inc(ln_step, 1)
                    for s in range(SUB):
                        dve.wait_ge(ln_step, at(b, 8 * NT, 8 * t + s + 1))
                        carry(k)
                        nc.vector.bn_aggr(mv[:, s, :], stats[:, s, :]).then_inc(ln_step, 1)
                    dve.wait_ge(rstd_ready, at(b, 2 * NT, 2 * t + 2))
                    dve.wait_ge(ln_step, at(b, 8 * NT, 8 * t + 8))
                    for s in range(SUB):
                        nc.vector.tensor_scalar(row(s), row(s), mv[:, s, 0:1], rstd[:, s:s + 1],
                                                ALU.subtract, ALU.mult).then_inc(normed, 1)
                    dve.wait_ge(normed, at(b, SUB * NT, SUB * (t + 1)))

                def group(r, b, g, last):
                    for t in range(NT):
                        if causal:
                            mask_diagonal(r, t)
                        dve.wait_ge(pv_done, at(r, NQ, last_quad[t] + 1))
                        dve.wait_ge(o_turned, at(r, NT, t - 1))
                        nc.vector.tensor_copy(o_sb[:, t % 2, :], ps[:, 6 + t % 2, :]).then_inc(o_copied, 1)
                        normalise(r, b, g, t)
                        if last and layer == 2:
                            last_norm(r, b, t)

                if causal:
                    dve.sem_inc(masked, 2 * NKB)
                    dve.wait_ge(consts, 16)
                if layer == 2:
                    dve.sem_inc(ln_step, 8 * NT)
                    dve.sem_inc(normed, SUB * NT)
                with rounds(k, mybir.EngineType.DVE, B) as b:
                    with rounds(k, mybir.EngineType.DVE, NG - 1) as g:
                        group(b * NG + g, b, g, False)
                    group(b * NG + (NG - 1), b, NG - 1, True)


def middle(k, weights):
    nc, ps = k.nc, k.ps
    a = k.a
    with ExitStack() as ctx:
        pr = Projection(k, ctx, 2, weights)
        wo, we = weights.wo, weights.we
        sb = lambda name, shape, dt: k.sb(name, shape, dt, ctx)
        be = sb("be", [E, D], F32)
        bv = sb("bv", [P, D], F32)
        bg = sb("bg", [P, SUB, E], F32)
        iota = sb("iota", [P, E], F32)
        xr = sb("xr", [P, 2, SUB, D], F32)
        att = sb("att", [P, SUB, D], F32)
        att_t = [sb(f"att_t_{n}", [P, C, QT], F32R) for n in ("high", "low")]
        x1 = sb("x1", [P, 2, SUB, D], F32)
        x1t = [sb(f"x1t_{n}", [P, 2, C, QT], F32R) for n in ("high", "low")]
        stats = sb("stats", [P, SUB, 6], F32)
        mv = sb("mv", [P, SUB, 2], F32)
        rstd = sb("rstd", [P, 2, SUB], F32)
        logit = sb("logit", [P, SUB, E], F32)
        small = sb("small", [P, SUB, 4], F32)
        expd = sb("expd", [P, SUB, E], F32)
        gate = sb("gate", [P, SUB, E], F32)
        top = sb("top", [P, SUB, E], F32)
        topi = sb("topi", [P, SUB, E], U32)
        topf = sb("topf", [P, SUB, E], F32)
        hot = sb("hot", [P, SUB, E], F32)
        comb = sb("comb", [P, 2, SUB, E], F32)
        comb_t = sb("comb_t", [E, QT], F32)
        consts = k.sem("middle_consts")
        x_loaded = [k.sem(f"residual_loaded{p}") for p in range(2)]
        att_copied = k.sem("att_copied")
        att_turned = k.sem("att_turned")
        att_high = k.sem("att_high")
        att_low = k.sem("att_low")
        o_ready = k.sem("o_ready")
        o_added = k.sem("o_added")
        ln_step = k.sem("ln_step")
        rstd_ready = k.sem("rstd_ready")
        x1_ready = k.sem("x1_ready")
        x1_turned = k.sem("x1_turned")
        x1_high = k.sem("x1_high")
        x1_low = k.sem("x1_low")
        gate_step = k.sem("gate_step")
        exp_ready = k.sem("exp_ready")
        comb_turned = k.sem("comb_turned")
        comb_copied = k.sem("comb_copied")
        be_ready = k.sem("be_ready")
        be_added = k.sem("be_added")
        exp_tile = k.sem("expert_tile")
        exp_added = k.sem("expert_added")
        half = NT // 2
        GS = 11 + 2 * SUB
        NE = E // 2

        def steps(engine, step):
            step(0, -1, False, True, True)
            with rounds(k, engine, B - 1) as r:
                for t in range(NT):
                    step(r, t, True, True, True)
            for t in range(NT):
                step(B - 1, t, True, t + 1 < NT, t + 2 < NT)

        def place(r, t):
            return r + t // NT, t % NT

        with nc.Block() as block:

            @block.sync
            def _(sp):
                pr.lead(sp, "sp")
                for s in x_loaded:
                    sp.sem_inc(s, 16 * half)
                src_x = a["x"].rearrange("b (n p) d -> p (b n) d", p=P)

                def load_x(r, t):
                    sp.dma_start(xr[:, t % 2, :, :], src_x[:, bass.ds(r * NKB + t * SUB, SUB), :]).then_inc(x_loaded[t % 2], 16)

                for t in range(2):
                    load_x(0, t)
                pr.sp_consts(sp)
                for dst, src in ((be[:, :], a["b_exp"]),
                                 (bv[:, :], a["b_qkv"][2 * D:3 * D].rearrange("(o n) -> o n", o=1).to_broadcast([P, D])),
                                 (iota[:, :], a["iota"])):
                    sp.dma_start(dst, src).then_inc(consts, 16)
                for s in range(SUB):
                    sp.dma_start(bg[:, s, :], a["b_gate"].rearrange("(o n) -> o n", o=1).to_broadcast([P, E])).then_inc(consts, 16)

                def step(r, t, now, next, after):
                    if next:
                        if not (isinstance(r, int) and r * NT + t + 3 >= N_BLOCKS):
                            alone(sp, k)
                            sp.wait_ge(x1_ready, at(r, SUB * NT, SUB * (t + 2)))
                            load_x(r, t + 3)
                        pr.sp_store(sp, *place(r, t + 1))
                    if now and t == NT - 1:
                        pr.sp_store_shift(sp, r)

                steps(mybir.EngineType.SP, step)
                pr.sp_end(sp)

            @block.gpsimd
            def _(pool):
                pool.sem_inc(att_copied, NT)
                pool.sem_inc(rstd_ready, 2 * NT)

                def copy_att(r, t):
                    pool.wait_ge(att_turned, at(r, NT, t))
                    nc.gpsimd.tensor_copy(att[:, :, :], k.tok[:, bass.ds(r * NKB + t * SUB, SUB), :]).then_inc(att_copied, 1)

                def roots(r, t):
                    pool.wait_ge(ln_step, at(r, 8 * NT, 8 * t + 8))
                    nc.gpsimd.tensor_tensor(rstd[:, 1, :], mv[:, :, 1], k.eps[:, :], ALU.add).then_inc(rstd_ready, 1)
                    pool.wait_ge(rstd_ready, at(r, 2 * NT, 2 * t + 1))
                    pool.wait_ge(x1_ready, at(r, SUB * NT, SUB * t))
                    nc.gpsimd.tensor_tensor(rstd[:, 0, :], rstd[:, 1, :], k.mhalf[:, :], ALU.pow).then_inc(rstd_ready, 1)

                def step(r, t, now, next, after):
                    if next:
                        roots(r, t + 1)
                    if after:
                        copy_att(r, t + 2)

                copy_att(0, 0)
                steps(mybir.EngineType.Pool, step)

            @block.tensor
            def _(pe):
                pr.lead(pe, "pe")
                for s, n in ((att_turned, NT), (o_ready, 2 * NT), (x1_turned, NT), (comb_turned, NT),
                             (be_ready, 2 * NT), (exp_tile, SUB * NE * NT)):
                    pe.sem_inc(s, n)
                pe.wait_ge(pr.consts, pr.n_consts)
                pe.wait_ge(consts, 16 * (3 + SUB))

                def turn(src, then):
                    for c in range(C):
                        for s in range(SUB):
                            last = nc.tensor.transpose(ps[:, 6 + c, s * P:(s + 1) * P], src[:, s, c * P:(c + 1) * P], k.ident[:, :])
                    last.then_inc(then, 1)

                def turn_att(r, t):
                    pe.wait_ge(att_copied, at(r, NT, t + 1))
                    pe.wait_ge(pr.v_copied, at(r, SUB * NT, SUB * t))
                    pe.wait_ge(gate_step, at(r, GS * NT, GS * (t - 1) + 1))
                    turn(att, att_turned)

                def out_projection(r, t):
                    pe.wait_ge(att_high, at(r, C * NT, C * (t + 1)))
                    pe.wait_ge(att_low, at(r, C * NT, C * (t + 1)))
                    for s in range(SUB):
                        last = product(k, ps[:, 4 + s // 2, s % 2 * D:(s % 2 + 1) * D], att_t, slice(s * P, (s + 1) * P),
                                       wo, slice(0, D))
                        if s % 2:
                            last.then_inc(o_ready, 1)

                def turn_x1(r, t):
                    pe.wait_ge(x1_ready, at(r, SUB * NT, SUB * (t + 1)))
                    pe.wait_ge(comb_copied, at(r, NT, t))
                    turn(x1[:, t % 2, :, :], x1_turned)

                def values_and_gate(r, t):
                    pe.wait_ge(x1_high, at(r, C * NT, C * (t + 1)))
                    pe.wait_ge(x1_low, at(r, C * NT, C * (t + 1)))
                    pe.wait_ge(o_added, at(r, 2 * NT, 2 * t + 2))
                    pe.wait_ge(be_added, at(r, 3 * NT, 3 * t))
                    pr.pe_v(pe, r, t, [x[:, t % 2, :, :] for x in x1t])

                def queries_and_keys(r, t):
                    pe.wait_ge(exp_added, at(r, SUB * E * NT, SUB * E * t))
                    pr.pe_tiles(pe, r, t, [x[:, t % 2, :, :] for x in x1t])

                def turn_weights(r, t):
                    pe.wait_ge(gate_step, at(r, GS * NT, GS * (t + 1)))
                    pe.wait_ge(pr.v_copied, at(r, SUB * NT, SUB * (t + 1)))
                    for s in range(SUB):
                        last = nc.tensor.transpose(ps[0:E, 6, s * P:(s + 1) * P], comb[:, t % 2, s, :], k.ident[:, :])
                    last.then_inc(comb_turned, 1)

                def biases(r, t, next):
                    pe.wait_ge(comb_copied, at(r, NT, t + 1))
                    if next:
                        pe.wait_ge(o_added, at(r, 2 * NT, 2 * t + 4))
                    for b in range(2):
                        for s in range(2):
                            last = nc.tensor.matmul(ps[:, 4 + b, s * D:(s + 1) * D],
                                                    comb_t[:, (2 * b + s) * P:(2 * b + s + 1) * P], be[:, :],
                                                    start=True, stop=True)
                        last.then_inc(be_ready, 1)

                def experts(r, t, s):
                    for e in range(NE):
                        n = s * NE + e
                        if n == 0:
                            pe.wait_ge(pr.qk_copied, at(r, 4 * NT, 4 * t + 4))
                        if n == 2:
                            pe.wait_ge(pr.norm_read, at(r, 2 * NT, 2 * t + 2))
                        if n >= 4:
                            pe.wait_ge(exp_added, at(r, SUB * E * NT, SUB * E * t + 2 * (n - 3)))
                        product(k, ps[:, n % 4, :], [x[:, t % 2, :, :] for x in x1t], slice(s * P, (s + 1) * P),
                                we, slice(2 * e * D, 2 * (e + 1) * D)).then_inc(exp_tile, 1)

                def step(r, t, now, next, after):
                    if now:
                        experts(r, t, 0)
                        biases(r, t, next)
                        experts(r, t, 1)
                    if next:
                        turn_x1(r, t + 1)
                    if now:
                        experts(r, t, 2)
                    if next:
                        values_and_gate(r, t + 1)
                    if now:
                        experts(r, t, 3)
                    if after:
                        turn_att(r, t + 2)
                    if next:
                        queries_and_keys(r, t + 1)
                    if after:
                        out_projection(r, t + 2)
                    if next:
                        turn_weights(r, t + 1)
                        pr.pe_norms(pe, *place(r, t + 1))

                turn_att(0, 0)
                out_projection(0, 0)
                steps(mybir.EngineType.PE, step)

            @block.scalar
            def _(act):
                pr.lead(act, "act")
                for s, n in ((att_high, C * NT), (x1_high, C * NT), (exp_ready, NT), (comb_copied, NT)):
                    act.sem_inc(s, n)
                act.wait_ge(pr.consts, pr.n_consts)

                def high_part(r, t, turned, dst, then):
                    act.wait_ge(turned, at(r, NT, t + 1))
                    for c in range(C):
                        nc.scalar.activation(dst[:, c, :], ps[:, 6 + c, :], ACT.Copy).then_inc(then, 1)

                def gate_exp(r, t):
                    act.wait_ge(gate_step, at(r, GS * NT, GS * t + 3))
                    nc.scalar.activation(expd[:, :, :], logit[:, :, :], ACT.Exp).then_inc(exp_ready, 1)

                def copy_weights(r, t):
                    act.wait_ge(comb_turned, at(r, NT, t + 1))
                    act.wait_ge(be_ready, at(r, 2 * NT, 2 * t))
                    nc.scalar.activation(comb_t[:, :], ps[0:E, 6, :], ACT.Copy).then_inc(comb_copied, 1)

                def step(r, t, now, next, after):
                    if next:
                        high_part(r, t + 1, x1_turned, x1t[0][:, (t + 1) % 2, :, :], x1_high)
                        gate_exp(r, t + 1)
                    if after:
                        high_part(r, t + 2, att_turned, att_t[0], att_high)
                    if next:
                        pr.act_tiles(act, r, t + 1)
                        copy_weights(r, t + 1)
                        if t + 1 == NT - 1:
                            pr.act_root(act, r)

                high_part(0, 0, att_turned, att_t[0], att_high)
                steps(mybir.EngineType.Activation, step)

            @block.vector
            def _(dve):
                nc.vector.memset(pr.v[:, :, :, DK:VW], 1.0).then_inc(pr.set, 1)
                dve.wait_ge(pr.set, 1)
                pr.lead(dve, "dve")
                for s, n in ((pr.v_copied, SUB * NT), (att_low, C * NT), (x1_low, C * NT), (o_added, 2 * NT),
                             (ln_step, 8 * NT), (x1_ready, SUB * NT), (gate_step, GS * NT), (be_added, 3 * NT),
                             (exp_added, SUB * E * NT)):
                    dve.sem_inc(s, n)
                dve.wait_ge(consts, 16 * (3 + SUB))

                def low_part(r, t, high_ready, dst, then):
                    for c in range(C):
                        dve.wait_ge(high_ready, at(r, C * NT, C * t + c + 1))
                        nc.vector.tensor_tensor(dst[1][:, c, :], ps[:, 6 + c, :], dst[0][:, c, :].bitcast(F32),
                                                ALU.subtract).then_inc(then, 1)

                def residual(r, t):
                    y = xr[:, t % 2, :, :]
                    rn, tn = place(r, t)
                    dve.wait_ge(x_loaded[t % 2], at(rn, 16 * half, 16 * (tn // 2 + 1)))
                    for b in range(2):
                        dve.wait_ge(o_ready, at(r, 2 * NT, 2 * t + b + 1))
                        nc.vector.tensor_tensor(y[:, 2 * b:2 * b + 2, :], ps[:, 4 + b, :].rearrange("p (s d) -> p s d", s=2),
                                                y[:, 2 * b:2 * b + 2, :], ALU.add).then_inc(o_added, 1)
                    for s in range(SUB):
                        dve.wait_ge(o_added, at(r, 2 * NT, 2 * t + s // 2 + 1))
                        nc.vector.bn_stats(stats[:, s, :], y[:, s, :]).then_inc(ln_step, 1)
                    dve.wait_ge(rstd_ready, at(r, 2 * NT, 2 * t))
                    for s in range(SUB):
                        dve.wait_ge(ln_step, at(r, 8 * NT, 8 * t + s + 1))
                        carry(k)
                        nc.vector.bn_aggr(mv[:, s, :], stats[:, s, :]).then_inc(ln_step, 1)

                def layer_norm(r, t):
                    dve.wait_ge(ln_step, at(r, 8 * NT, 8 * t + 8))
                    dve.wait_ge(rstd_ready, at(r, 2 * NT, 2 * t + 2))
                    dve.wait_ge(exp_added, at(r, SUB * E * NT, SUB * E * (t - 1)))
                    for s in range(SUB):
                        nc.vector.tensor_scalar(x1[:, t % 2, s, :], xr[:, t % 2, s, :], mv[:, s, 0:1], rstd[:, 0, s:s + 1],
                                                ALU.subtract, ALU.mult).then_inc(x1_ready, 1)

                spread = lambda x: x.unsqueeze(2).to_broadcast([P, SUB, E])

                def stepper(r, t, done):
                    count = [done]

                    def step(ins, wait=True):
                        count[0] += 1
                        ins.then_inc(gate_step, 1)
                        if wait:
                            dve.wait_ge(gate_step, at(r, GS * NT, GS * t + count[0]))
                    return step

                def logits_and_values(r, t):
                    step, wide = stepper(r, t, 0), spread
                    dve.wait_ge(pr.v_ready, at(r, SUB * NT, SUB * (t + 1)))
                    step(nc.vector.tensor_tensor(logit[:, :, :], ps[:, 4:8, D:D + E], bg[:, :, :], ALU.add))
                    step(nc.vector.tensor_reduce(small[:, :, 0], logit[:, :, :], AX.X, ALU.max))
                    step(nc.vector.tensor_tensor(logit[:, :, :], logit[:, :, :], wide(small[:, :, 0]), ALU.subtract))
                    pr.dve_v(dve, r, t, bv)

                def gating(r, t):
                    step, wide = stepper(r, t, 3), spread
                    dve.wait_ge(exp_ready, at(r, NT, t + 1))
                    step(nc.vector.tensor_reduce(small[:, :, 1], expd[:, :, :], AX.X, ALU.add))
                    step(nc.vector.reciprocal(small[:, :, 2], small[:, :, 1]))
                    step(nc.vector.tensor_tensor(gate[:, :, :], expd[:, :, :], wide(small[:, :, 2]), ALU.mult))
                    carry(k)
                    for s in range(SUB):
                        step(nc.vector.max(top[:, s, :], gate[:, s, :]), s == SUB - 1)
                    carry(k)
                    for s in range(SUB):
                        step(nc.vector.max_index(topi[:, s, :], top[:, s, :], gate[:, s, :]), s == SUB - 1)
                    step(nc.vector.tensor_copy(topf[:, :, :], topi[:, :, :]))
                    io = iota[:, :].unsqueeze(1).to_broadcast([P, SUB, E])
                    step(nc.vector.tensor_tensor(hot[:, :, :], io, wide(topf[:, :, 0]), ALU.is_equal), False)
                    step(nc.vector.tensor_tensor(logit[:, :, :], io, wide(topf[:, :, 1]), ALU.is_equal))
                    step(nc.vector.tensor_tensor(hot[:, :, :], hot[:, :, :], logit[:, :, :], ALU.add))
                    step(nc.vector.tensor_tensor(comb[:, t % 2, :, :], hot[:, :, :], gate[:, :, :], ALU.mult))

                def add_biases(r, t):
                    acc = x1[:, t % 2, :, :]
                    bias = ps[:, 4:6, :].rearrange("p b (s d) -> p (b s) d", s=2)
                    dve.wait_ge(be_ready, at(r, 2 * NT, 2 * t + 1))
                    dve.wait_ge(exp_added, at(r, SUB * E * NT, SUB * E * t + E))
                    nc.vector.tensor_tensor(k.tok[:, bass.ds(r * NKB + t * SUB, 1), :], bias[:, 0:1, :], acc[:, 0:1, :],
                                            ALU.add).then_inc(be_added, 1)
                    nc.vector.tensor_tensor(acc[:, 1, :], bias[:, 1, :], acc[:, 1, :], ALU.add).then_inc(be_added, 1)
                    dve.wait_ge(be_ready, at(r, 2 * NT, 2 * t + 2))
                    nc.vector.tensor_tensor(acc[:, 2:4, :], bias[:, 2:4, :], acc[:, 2:4, :], ALU.add).then_inc(be_added, 1)

                def add_experts(r, t, s):
                    acc = x1[:, t % 2, :, :]
                    if s:
                        dve.wait_ge(be_added, at(r, 3 * NT, 3 * t + min(s, 2) + 1))
                    for e in range(E):
                        n = s * E + e
                        dve.wait_ge(exp_tile, at(r, SUB * NE * NT, SUB * NE * t + n // 2 + 1))
                        if e:
                            dve.wait_ge(exp_added, at(r, SUB * E * NT, SUB * E * t + n))
                        dst = acc[:, s, :]
                        if s and e == E - 1:
                            dst = k.tok[:, bass.ds(r * NKB + t * SUB + s, 1), :].rearrange("p o d -> p (o d)")
                        nc.vector.scalar_tensor_tensor(dst, ps[:, (n // 2) % 4, (n % 2) * D:(n % 2 + 1) * D],
                                                       comb[:, t % 2, s, e:e + 1], acc[:, s, :], ALU.mult,
                                                       ALU.add).then_inc(exp_added, 1)

                def step(r, t, now, next, after):
                    if next:
                        residual(r, t + 1)
                    if now:
                        add_experts(r, t, 0)
                    if next:
                        layer_norm(r, t + 1)
                    if now:
                        if t == NT - 1:
                            pr.dve_shift(dve, r)
                        add_biases(r, t)
                        add_experts(r, t, 1)
                    if next:
                        low_part(r, t + 1, x1_high, [x[:, (t + 1) % 2, :, :] for x in x1t], x1_low)
                    if now:
                        add_experts(r, t, 2)
                    if next:
                        logits_and_values(r, t + 1)
                    if now:
                        add_experts(r, t, 3)
                    if after:
                        low_part(r, t + 2, att_high, att_t, att_low)
                    if next:
                        gating(r, t + 1)
                        pr.dve_split(dve, *place(r, t + 1))
                        pr.dve_norms(dve, *place(r, t + 1))

                low_part(0, 0, att_high, att_t, att_low)
                steps(mybir.EngineType.DVE, step)
                pr.dve_flag(dve)


def program(nc, args, out):
    with ExitStack() as ctx:
        k = Build(nc, ctx, args, out)
        start(k)
        project(k)
        row_max(k, 1)
        with ExitStack() as held:
            weights = Weights(k, held, 2)
            attend(k, 1, weights)
            middle(k, weights)
        row_max(k, 2)
        attend(k, 2)


def kernel(L0_attn_X, L0_attn_q_proj, L0_attn_k_proj, L0_attn_v_proj, L0_attn_o_proj, L0_ffn_W_qkv, L0_ffn_b_qkv,
           L0_ffn_W_gate, L0_ffn_b_gate, L0_ffn_W_experts, L0_ffn_b_experts):
    import concourse.bacc as _bacc
    import ml_dtypes
    from concourse.bass_utils import run_bass_kernel_spmd as _run

    lay = np.ascontiguousarray
    x = np.asarray(L0_attn_X)
    head_of = np.arange(P)[:, None] // DK == np.arange(32)[None, :]
    bf = ml_dtypes.bfloat16
    arrays = {
        "x": x,
        "xt": lay(np.swapaxes(x, 1, 2)),
        "wqkv1": lay(np.concatenate([np.asarray(w).T for w in (L0_attn_q_proj, L0_attn_k_proj, L0_attn_v_proj)], axis=1)),
        "wo": lay(np.asarray(L0_attn_o_proj).T),
        "wqkv2": lay(np.concatenate([np.asarray(L0_ffn_W_qkv), np.asarray(L0_ffn_W_gate)], axis=1)),
        "b_qkv": np.asarray(L0_ffn_b_qkv),
        "b_gate": np.asarray(L0_ffn_b_gate),
        "w_exp": np.asarray(L0_ffn_W_experts),
        "b_exp": np.asarray(L0_ffn_b_experts),
        "ident": np.eye(P, dtype=np.float32),
        "mask": np.where(np.arange(P)[:, None] > np.arange(P)[None, :], 0.0, 3e38).astype(np.float32),
        "mask_wide": np.where(np.arange(QT)[None, None, :] > np.arange(P)[:, None, None] + P * np.arange(SUB)[None, :, None],
                              MASK, 0.0).astype(np.float32),
        "iota": np.tile(np.arange(E, dtype=np.float32), (P, 1)),
        "sums": (head_of * MARGIN).astype(bf),
    }
    nc = _bacc.Bacc("TRN2", target_bir_lowering=False, num_devices=1)
    args = {n: nc.dram_tensor(f"in_{n}", v.shape, mybir.dt.from_np(v.dtype), kind="ExternalInput").ap()
            for n, v in arrays.items()}
    out = nc.dram_tensor("out_0", (B, S, D), F32, kind="ExternalOutput").ap()
    program(nc, args, out)
    r = _run(nc, [{f"in_{n}": v for n, v in arrays.items()}], core_ids=[0])
    return r.results[0]["out_0"]
```
